# Optimizing a Trainium2 kernel written in Bass

```python
import numpy as np
import jax
import jax.numpy as jnp

def _softmax(x, axis=-1):
    return jax.nn.softmax(x, axis=axis)

def _gelu(x):
    return jax.nn.gelu(x, approximate=True)

def _silu(x):
    return jax.nn.silu(x)

def _sigmoid(x):
    return jax.nn.sigmoid(x)

def _layernorm(x, axis=-1, eps=1e-05):
    m = jnp.mean(x, axis=axis, keepdims=True)
    v = jnp.var(x, axis=axis, keepdims=True)
    return (x - m) / jnp.sqrt(v + eps)

def _scatter_add(tgt, idx, src, axis=0):
    return tgt.at[idx].add(src)

def _segment_sum(src, seg, n):
    return jax.ops.segment_sum(src, seg, n)
kernel_name = 'mk_recurrent_d1_jaxref_r2_92911a'

def setup_inputs(seed: int=0):
    np.random.seed(seed)
    _w = jnp.asarray

    def _L0_attn_setup():
        import jax, jax.numpy as jnp
        import numpy as np
        import math
        B, T, C = (2, 1024, 1024)
        N_HEAD = 16
        N_KV = 4
        GROUP = N_HEAD // N_KV
        HS = C // N_HEAD
        WINDOW = 512
        SINK = 4

        def _sliding_window_sink_mask(t):
            i = jnp.arange(t)[:, None]
            j = jnp.arange(t)[None, :]
            causal = j <= i
            band = j >= i - (WINDOW - 1)
            mask = causal & band
            mask = mask | (j < SINK)
            mask = mask & ((i >= SINK) | causal)
            return mask
        key = jax.random.key(seed)
        ks = jax.random.split(key, 5)
        s = 1.0 / math.sqrt(C)
        return {'x': jax.random.normal(ks[0], (B, T, C), dtype=jnp.float32), 'Wq': jax.random.normal(ks[1], (C, C), dtype=jnp.float32) * s, 'Wk': jax.random.normal(ks[2], (N_KV * HS, C), dtype=jnp.float32) * s, 'Wv': jax.random.normal(ks[3], (N_KV * HS, C), dtype=jnp.float32) * s, 'Wo': jax.random.normal(ks[4], (C, C), dtype=jnp.float32) * s}
    _L0_attn_in = _L0_attn_setup()

    def _L0_ffn_setup():
        import jax, jax.numpy as jnp
        import numpy as np
        EPS = 1e-06
        K_STEPS = 4
        USE_GATING = True

        def layer_norm(x, gamma, beta):
            mu = jnp.mean(x, axis=-1, keepdims=True)
            var = jnp.mean(jnp.square(x - mu), axis=-1, keepdims=True)
            return (x - mu) * jax.lax.rsqrt(var + EPS) * gamma + beta
        key = jax.random.key(seed)
        B, L, D, H = (4, 2048, 1024, 4096)
        ks = jax.random.split(key, 16)
        s = 0.02
        return {'x': jax.random.normal(ks[0], (B, L, D), dtype=jnp.float32), 'in_gamma': jnp.ones((D,), jnp.float32), 'in_beta': jnp.zeros((D,), jnp.float32), 'agg_w': jax.random.normal(ks[1], (D, D), jnp.float32) * s, 'agg_b': jnp.zeros((D,), jnp.float32), 'pn_gamma': jnp.ones((D,), jnp.float32), 'pn_beta': jnp.zeros((D,), jnp.float32), 'd1_w': jax.random.normal(ks[2], (D, H), jnp.float32) * s, 'd1_b': jnp.zeros((H,), jnp.float32), 'd2_w': jax.random.normal(ks[3], (H, D), jnp.float32) * s, 'd2_b': jnp.zeros((D,), jnp.float32), 'bc_w': jax.random.normal(ks[4], (D, D), jnp.float32) * s, 'bc_b': jnp.zeros((D,), jnp.float32), 'gate_w': jax.random.normal(ks[5], (D, D), jnp.float32) * s, 'gate_b': jnp.zeros((D,), jnp.float32), 'out_gamma': jnp.ones((D,), jnp.float32), 'out_beta': jnp.zeros((D,), jnp.float32)}
    _L0_ffn_in = _L0_ffn_setup()
    _d = {'L0_attn_x': _L0_attn_in['x'], 'L0_attn_Wq': _L0_attn_in['Wq'], 'L0_attn_Wk': _L0_attn_in['Wk'], 'L0_attn_Wv': _L0_attn_in['Wv'], 'L0_attn_Wo': _L0_attn_in['Wo'], 'L0_ffn_in_gamma': _L0_ffn_in['in_gamma'], 'L0_ffn_in_beta': _L0_ffn_in['in_beta'], 'L0_ffn_agg_w': _L0_ffn_in['agg_w'], 'L0_ffn_agg_b': _L0_ffn_in['agg_b'], 'L0_ffn_pn_gamma': _L0_ffn_in['pn_gamma'], 'L0_ffn_pn_beta': _L0_ffn_in['pn_beta'], 'L0_ffn_d1_w': _L0_ffn_in['d1_w'], 'L0_ffn_d1_b': _L0_ffn_in['d1_b'], 'L0_ffn_d2_w': _L0_ffn_in['d2_w'], 'L0_ffn_d2_b': _L0_ffn_in['d2_b'], 'L0_ffn_bc_w': _L0_ffn_in['bc_w'], 'L0_ffn_bc_b': _L0_ffn_in['bc_b'], 'L0_ffn_gate_w': _L0_ffn_in['gate_w'], 'L0_ffn_gate_b': _L0_ffn_in['gate_b'], 'L0_ffn_out_gamma': _L0_ffn_in['out_gamma'], 'L0_ffn_out_beta': _L0_ffn_in['out_beta']}
    _x0 = _d['L0_attn_x']
    _d['L0_attn_x'] = jax.random.normal(jax.random.fold_in(jax.random.key(seed), 1), (4, 1024, 1024), dtype=_x0.dtype)
    del _x0
    return _d

def reference(L0_attn_x, L0_attn_Wq, L0_attn_Wk, L0_attn_Wv, L0_attn_Wo, L0_ffn_in_gamma, L0_ffn_in_beta, L0_ffn_agg_w, L0_ffn_agg_b, L0_ffn_pn_gamma, L0_ffn_pn_beta, L0_ffn_d1_w, L0_ffn_d1_b, L0_ffn_d2_w, L0_ffn_d2_b, L0_ffn_bc_w, L0_ffn_bc_b, L0_ffn_gate_w, L0_ffn_gate_b, L0_ffn_out_gamma, L0_ffn_out_beta):

    def _L0_attn_ref(x, Wq, Wk, Wv, Wo):
        import jax, jax.numpy as jnp
        import numpy as np
        import math
        B, T, C = (2, 1024, 1024)
        N_HEAD = 16
        N_KV = 4
        GROUP = N_HEAD // N_KV
        HS = C // N_HEAD
        WINDOW = 512
        SINK = 4

        def _sliding_window_sink_mask(t):
            i = jnp.arange(t)[:, None]
            j = jnp.arange(t)[None, :]
            causal = j <= i
            band = j >= i - (WINDOW - 1)
            mask = causal & band
            mask = mask | (j < SINK)
            mask = mask & ((i >= SINK) | causal)
            return mask
        b, t, c = x.shape
        q = (x @ Wq.T).reshape(b, t, N_HEAD, HS).transpose(0, 2, 1, 3)
        q = q.reshape(b, N_KV, GROUP, t, HS)
        k = (x @ Wk.T).reshape(b, t, N_KV, HS).transpose(0, 2, 1, 3)
        v = (x @ Wv.T).reshape(b, t, N_KV, HS).transpose(0, 2, 1, 3)
        scale = 1.0 / math.sqrt(HS)
        att = jnp.einsum('bkgqd,bkjd->bkgqj', q, k) * scale
        mask = _sliding_window_sink_mask(t)
        att = jnp.where(mask[None, None, None, :, :], att, -jnp.inf)
        att = jax.nn.softmax(att, axis=-1)
        y = jnp.einsum('bkgqj,bkjd->bkgqd', att, v)
        y = y.reshape(b, N_HEAD, t, HS).transpose(0, 2, 1, 3).reshape(b, t, c)
        return y @ Wo.T

    def _L0_ffn_ref(x, in_gamma, in_beta, agg_w, agg_b, pn_gamma, pn_beta, d1_w, d1_b, d2_w, d2_b, bc_w, bc_b, gate_w, gate_b, out_gamma, out_beta):
        import jax, jax.numpy as jnp
        import numpy as np
        EPS = 1e-06
        K_STEPS = 4
        USE_GATING = True

        def layer_norm(x, gamma, beta):
            mu = jnp.mean(x, axis=-1, keepdims=True)
            var = jnp.mean(jnp.square(x - mu), axis=-1, keepdims=True)
            return (x - mu) * jax.lax.rsqrt(var + EPS) * gamma + beta
        x_norm = layer_norm(x, in_gamma, in_beta)
        thought = x_norm[:, -1, :] @ agg_w + agg_b
        for _ in range(K_STEPS):
            t = layer_norm(thought, pn_gamma, pn_beta)
            t = jax.nn.gelu(t @ d1_w + d1_b, approximate=False)
            thought = thought + (t @ d2_w + d2_b)
        broadcast = (thought @ bc_w + bc_b)[:, None, :]
        if USE_GATING:
            gate = jax.nn.sigmoid(x @ gate_w + gate_b)
            out = x + gate * broadcast
        else:
            out = x + broadcast
        return layer_norm(out, out_gamma, out_beta)
    x = L0_attn_x
    xn = _layernorm(x, axis=-1)
    s = _L0_attn_ref(xn, L0_attn_Wq, L0_attn_Wk, L0_attn_Wv, L0_attn_Wo)
    g = _silu(_L0_ffn_ref(xn, L0_ffn_in_gamma, L0_ffn_in_beta, L0_ffn_agg_w, L0_ffn_agg_b, L0_ffn_pn_gamma, L0_ffn_pn_beta, L0_ffn_d1_w, L0_ffn_d1_b, L0_ffn_d2_w, L0_ffn_d2_b, L0_ffn_bc_w, L0_ffn_bc_b, L0_ffn_gate_w, L0_ffn_gate_b, L0_ffn_out_gamma, L0_ffn_out_beta))
    x = x + s * g
    return x

_drawn_inputs = setup_inputs


def setup_inputs(seed=0):
    import zlib

    import numpy as np

    out = dict(_drawn_inputs(seed))
    spreads = {'L0_ffn_in_gamma': (1.0, 0.6),
     'L0_ffn_in_beta': (0.0, 2.0),
     'L0_ffn_agg_b': (0.0, 0.8),
     'L0_ffn_pn_gamma': (1.0, 0.6),
     'L0_ffn_pn_beta': (0.0, 0.8),
     'L0_ffn_d1_b': (0.0, 0.8),
     'L0_ffn_d2_b': (0.0, 0.622),
     'L0_ffn_bc_b': (0.0, 0.8),
     'L0_ffn_gate_b': (0.0, 2.0),
     'L0_ffn_out_gamma': (1.0, 0.6),
     'L0_ffn_out_beta': (0.0, 0.8)}
    factors = {'L0_ffn_gate_w': 3.553}
    for name, (base, spread) in spreads.items():
        noise = np.random.default_rng([zlib.crc32(name.encode()), seed]).standard_normal(out[name].shape)
        drawn = base * np.exp(spread * noise) if base else spread * noise
        out[name] = jnp.asarray(drawn.astype(out[name].dtype))
    for name, factor in factors.items():
        out[name] = (out[name] * factor).astype(out[name].dtype)
    return out
```

```python
from contextlib import ExitStack

import concourse.bass as bass
from concourse import mybir

F32 = mybir.dt.float32
F32R = mybir.dt.float32r
ACT = mybir.ActivationFunctionType
ALU = mybir.AluOpType
AX = mybir.AxisListType

P = 128
B, T, C = 4, 1024, 1024
HEADS, KV, HS = 16, 4, 64
WINDOW, SINK = 512, 4
HID = 4096
KB = C // P
TB = T // P
HB = HID // P
BANK = 512
WB = WINDOW // P
WIDE = (WB + 1) * P
PAIRS = HEADS // 2
NEG = -3.0e38
SCALE = HS ** -0.5
EPS_X, EPS_FFN = 1e-5, 1e-6
Q_TILES, K_TILES, V_TILES, O_TILES = 8, 2, 2, 8
K0 = Q_TILES
V0 = K0 + K_TILES
O0 = V0 + V_TILES
GROUPS = KV
UNITS = 2 * 2 * TB
FW_BLOCKS = 4
FW_TILES = 8




def start_counted(eng, *sems, dma=False):
    for s in sems:
        eng.sem_inc(s, 16 if dma else 1)


def after(n):
    return n + 1


def landed(n):
    return 16 * n + 16


def blocks_of(qb):
    return min(qb + 1, WB + 1)


class LayerNormStats:

    def __init__(self, stats_done, var_done, rstd_done, eps_added, wait_over):
        self.wait_over = wait_over
        self.stats_done, self.var_done = stats_done, var_done
        self.rstd_done, self.eps_added = rstd_done, eps_added


def ln_statistics(dve, ln, n, src, rows, st, mv):
    for half in range(2):
        last = dve.bn_stats(st[0:rows, half, :], src[:, half * BANK:(half + 1) * BANK])
    last.then_inc(ln.stats_done, 1)
    dve.wait_ge(ln.stats_done, n + 1)
    dve.sem_inc(ln.wait_over, 1)
    dve.bn_aggr(mv[0:rows, :], st[0:rows, :, :]).then_inc(ln.var_done, 1)


def ln_rstd(pool, ln, n, mv, rstd, rows, eps, minus_half):
    pool.wait_ge(ln.var_done, n + 1)
    pool.tensor_tensor(rstd[0:rows, 1:2], mv[0:rows, 1:2], eps[0:rows, :], ALU.add).then_inc(ln.eps_added, 1)
    pool.wait_ge(ln.eps_added, n + 1)
    pool.tensor_tensor(rstd[0:rows, 0:1], rstd[0:rows, 1:2], minus_half[0:rows, :],
                       ALU.pow).then_inc(ln.rstd_done, 1)


def ln_apply(dve, ln, n, dst, src, mv, rstd, rows):
    dve.wait_ge(ln.rstd_done, n + 1)
    return dve.tensor_scalar(dst, src, mv[0:rows, 0:1], rstd[0:rows, 0:1], ALU.subtract, ALU.mult)


def prepare_weights(nc, WT, Wq, Wk, Wv, Wo):
    with ExitStack() as ctx:
        def sb(name, shape, dt):
            return ctx.enter_context(nc.sbuf_tensor(name, shape, dt))

        def sem(name):
            return ctx.enter_context(nc.semaphore(name))

        raw = [sb(f"w_raw{s}", [P, C], F32) for s in range(2)]
        split = [sb(f"w_split{s}", [P, 2, C], F32R) for s in range(2)]
        ident = sb("w_ident", [P, P], F32)
        turned = [ctx.enter_context(nc.psum_tensor(f"w_turned{s}", [P, C], F32)) for s in range(2)]
        zeroed, ident_ready = sem("w_zeroed"), sem("w_ident_ready")
        raw_loaded = [sem(f"w_raw_loaded{s}") for s in range(2)]
        split_stored = [sem(f"w_split_stored{s}") for s in range(2)]
        transposed, hi_ready, lo_ready = sem("w_transposed"), sem("w_hi_ready"), sem("w_lo_ready")

        weights = [(Wq, 0, Q_TILES), (Wk, K0, K_TILES), (Wv, V0, V_TILES), (Wo, O0, O_TILES)]

        def each_tile(eng, body):
            for W, first, count in weights:
                if count == 2:
                    for s in range(2):
                        body(W, s, first + s, s, first // 2)
                else:
                    with eng.Fori(0, count // 2) as i:
                        for s in range(2):
                            body(W, 2 * i + s, first + 2 * i + s, s, i + first // 2)

        with nc.Block() as block:
            @block.sync
            def _(sp):
                start_counted(sp, *split_stored, dma=True)

                def pair(W, i, first, turn):
                    for s in range(2):
                        if s == 0:
                            sp.wait_ge(transposed, after(2 * turn))
                        sp.dma_start(raw[s][:, :], W[bass.ts(2 * i + s, P), :]).then_inc(raw_loaded[s], 16)
                    for s in range(2):
                        sp.wait_ge(lo_ready, after(2 * turn + s + 1))
                        sp.dma_start(WT[first + 2 * i + s, :, :],
                                     split[s][:, :, :].rearrange("p a n -> p (a n)").bitcast(F32)).then_inc(
                            split_stored[s], 16)

                for W, first, count in weights:
                    if count == 2:
                        pair(W, 0, first, first // 2)
                    else:
                        with sp.Fori(0, count // 2) as i:
                            pair(W, i, first, i + first // 2)
                for s in range(2):
                    sp.wait_ge(split_stored[s], landed((O0 + O_TILES) // 2))

            @block.gpsimd
            def _(pool):
                pool.memset(ident[:, :], 0.0).then_inc(zeroed, 1)
                pool.wait_ge(zeroed, 1)
                pool.affine_select(out=ident[:, :], in_=ident[:, :], compare_op=ALU.not_equal, fill=1.0,
                                   base=0, pattern=[[-1, P]], channel_multiplier=1).then_inc(ident_ready, 1)

            @block.tensor
            def _(pe):
                start_counted(pe, transposed)
                pe.wait_ge(ident_ready, 1)

                def tile(W, row, t, s, turn):
                    pe.wait_ge(raw_loaded[s], 16 * turn + 16)
                    pe.wait_ge(lo_ready, after(2 * turn))
                    for c in range(KB):
                        last = pe.transpose(turned[s][:, bass.ts(c, P)], raw[s][:, bass.ts(c, P)], ident[:, :])
                    last.then_inc(transposed, 1)
                each_tile(pe, tile)

            @block.scalar
            def _(act):
                def tile(W, row, t, s, turn):
                    act.wait_ge(transposed, after(2 * turn + s + 1))
                    act.wait_ge(split_stored[s], landed(turn))
                    act.activation(split[s][:, 0, :], turned[s][:, :], ACT.Copy).then_inc(hi_ready, 1)
                each_tile(act, tile)

            @block.vector
            def _(dve):
                start_counted(dve, lo_ready)

                def tile(W, row, t, s, turn):
                    dve.wait_ge(hi_ready, 2 * turn + s + 1)
                    dve.tensor_tensor(split[s][:, 1, :], turned[s][:, :], split[s][:, 0, :].bitcast(F32),
                                      ALU.subtract).then_inc(lo_ready, 1)
                each_tile(dve, tile)


def attend(nc, WT, Y, BC, x, in_gamma, in_beta, agg_w, agg_b, pn_gamma, pn_beta, d1_w, d1_b, d2_w, d2_b,
           bc_w, bc_b):
    with ExitStack() as ctx:
        def sb(name, shape, dt=F32):
            return ctx.enter_context(nc.sbuf_tensor(name, shape, dt))

        def ps(name, cols):
            return ctx.enter_context(nc.psum_tensor(name, [P, cols], F32))

        def sem(name):
            return ctx.enter_context(nc.semaphore(name))

        xn = [sb(f"xn{s}", [P, C]) for s in range(2)]
        x_hi = sb("x_hi", [P, KB, T], F32R)
        x_lo = sb("x_lo", [P, KB, T], F32R)
        w = sb("w", [P, 4, 2 * C], F32R)
        k_hi = sb("k_hi", [P, KV, T], F32R)
        k_lo = sb("k_lo", [P, KV, T], F32R)
        v = sb("v", [P, TB, KV, HS + 1])
        q = [sb(f"q{n}", [P, T], F32R) for n in range(4)]
        probs = [sb(f"probs{n}", [P, WIDE + SINK]) for n in range(3)]
        probs_t = [sb(f"probs_t{n}", [P, WIDE + P]) for n in range(2)]
        mask = sb("mask", [P, WIDE + SINK])
        mask4 = sb("mask4", [P, WIDE])
        y = [sb(f"y{n}", [P, 2, HS]) for n in range(2)]
        neg_max = sb("neg_max", [P, 4])
        inv_sum = sb("inv_sum", [P, 2, 2])
        ident = sb("ident", [P, P])
        fold = sb("fold", [P, B])
        st = [sb(f"st{s}", [P, 2, 6]) for s in range(2)]
        mv = [sb(f"mv{s}", [P, 2]) for s in range(2)]
        rstd = [sb(f"rstd{s}", [P, 2]) for s in range(2)]
        eps_x, eps_ffn, minus_half = sb("eps_x", [P, 1]), sb("eps_ffn", [P, 1]), sb("minus_half", [P, 1])
        fw = [sb(f"fw{s}", [P, FW_BLOCKS, BANK]) for s in range(2)]
        rows = sb("rows", [P, BANK])
        ffn_rows = sb("ffn_rows", [P, C])
        thought = ffn_rows[0:B, :]
        t_rows = ffn_rows[32:32 + B, :]
        bias_rows = ffn_rows[64:64 + B, :]
        affine = sb("affine", [P, 4, KB])
        d1_bias = sb("d1_bias", [P, HB])
        h_pre = sb("h_pre", [P, HB, B])
        cols = sb("cols", [P, HB, 32])

        s_ps = [ps(f"s_ps{n}", 2 * BANK) for n in range(2)]
        t_ps = ps("t_ps", 2 * BANK)
        o_ps = ps("o_ps", BANK)
        j_ps = ps("j_ps", BANK)
        o_view = o_ps[:, 0:2 * (HS + 1)].rearrange("p (h d) -> p h d", h=2)
        f_cols = j_ps[:, 0:KB * B]
        f_hid = j_ps[:, 0:4 * B].rearrange("p (n b) -> p n b", b=B)

        small_loaded = sem("small_loaded")
        bias_loaded = sem("bias_loaded")
        last_loaded = sem("last_loaded")
        x_loaded = [sem(f"x_loaded{s}") for s in range(2)]
        w_loaded = [sem(f"w_loaded{s}") for s in range(4)]
        fw_loaded = [sem(f"fw_loaded{s}") for s in range(2)]
        y_stored = [sem(f"y_stored{n}") for n in range(2)]
        bc_stored = sem("bc_stored")
        filled, masks_ready, ident_ready, fold_ready = (sem("filled"), sem("masks_ready"), sem("ident_ready"),
                                                        sem("fold_ready"))
        ln = LayerNormStats(sem("ln_stats"), sem("ln_var"), sem("ln_rstd"), sem("ln_eps"), sem("ln_wait_over"))
        xn_ready, x_turned, x_hi_ready, x_lo_ready = sem("xn_ready"), sem("x_turned"), sem("x_hi_r"), sem("x_lo_r")
        k_full, k_hi_ready, k_lo_ready = sem("k_full"), sem("k_hi_r"), sem("k_lo_r")
        v_full, v_ready = sem("v_full"), sem("v_ready")
        q_full, q_hi_ready, q_lo_ready = sem("q_full"), sem("q_hi_r"), sem("q_lo_r")
        scores_ready, masked, exp_done = sem("scores_ready"), sem("masked"), sem("exp_done")
        turned, copied_a, copied_b = sem("turned"), sem("copied_a"), sem("copied_b")
        pv_done, inv_ready, y_ready = sem("pv_done"), sem("inv_ready"), sem("y_ready")
        fw_used, rows_ready, f_turned = sem("fw_used"), sem("rows_ready"), sem("f_turned")
        t_rows_ready, cols_ready, cols_scaled = sem("t_rows_ready"), sem("cols_ready"), sem("cols_scaled")
        hid_turned, hid_ready, gelu_done = sem("hid_turned"), sem("hid_ready"), sem("gelu_done")
        folded, biased, thought_ready = sem("folded"), sem("biased"), sem("thought_ready")
        last_normed, rows_zeroed, wait_over = sem("last_normed"), sem("rows_zeroed"), sem("wait_over")

        d1_view = d1_w.rearrange("(h k p) n -> h p k n", k=FW_BLOCKS, p=P)
        d2_view = d2_w.rearrange("(h k p) n -> h p k n", k=FW_BLOCKS, p=P)
        agg_view = agg_w.rearrange("(h k p) n -> h p k n", k=FW_BLOCKS, p=P)
        bc_view = bc_w.rearrange("(h k p) n -> h p k n", k=FW_BLOCKS, p=P)

        def unit(u):
            return u // (2 * TB), (u // 2) % TB, u % 2

        wide = [0] * (UNITS + 1)
        for u in range(UNITS):
            wide[u + 1] = wide[u] + (blocks_of(unit(u)[1]) > WB)
        HIDDEN_TILE = {16 + 4 * n + r: 2 * n + r for n in range(4) for r in range(2)}
        OUTPUT_TILE = {17 + 2 * t: t for t in range(FW_TILES)}

        def ffn_tile(layer, u):
            return (HIDDEN_TILE if layer == 0 else OUTPUT_TILE).get(u)

        FW_FIRST = 4
        Q_LNS = 2
        LNS = TB + 1

        def chunks_before(b, layer, j):
            return 2 + b * 10 + (4 * j if layer == 0 else 8 + j)

        def loops(eng, start, hidden_start, output_start, body, end=None):
            with eng.Fori(0, B) as b:
                start(b)
                for layer in range(2):
                    if layer == 0:
                        hidden_start(b)
                    else:
                        output_start(b)
                    with eng.Fori(0, 2) as j:
                        body(b, layer, j, 2 * layer + j, 4 * b + 2 * layer + j)

        def nothing(b):
            return None

        with nc.Block() as block:
            @block.sync
            def _(sp):
                start_counted(sp, *y_stored, dma=True)
                with nc.allow_non_contiguous_dma(reason="small vectors, one element per partition"):
                    for n, vec in enumerate((in_gamma, in_beta, pn_gamma, pn_beta)):
                        sp.dma_start(affine[:, n, :], vec.rearrange("(k p) -> p k", p=P)).then_inc(small_loaded, 16)
                    sp.dma_start(d1_bias[:, :], d1_b.rearrange("(k p) -> p k", p=P)).then_inc(small_loaded, 16)
                sp.wait_ge(rows_zeroed, 1)
                sp.dma_start(thought[:, :], x[:, T - 1, :]).then_inc(last_loaded, 16)
                sp.dma_start(bias_rows[:, :], agg_b.partition_broadcast(B)).then_inc(bias_loaded, 16)
                for s in range(4):
                    sp.dma_start(w[:, s, :].bitcast(F32), WT[K0 + s, :, :]).then_inc(w_loaded[s], 16)

                def fw_load(view, n, half, count):
                    s = n % 2
                    sp.wait_ge(fw_used, count - 1)
                    sp.dma_start(fw[s][:, :, :], view[half, :, :, bass.ts(n_col[0], BANK)]).then_inc(fw_loaded[s], 16)

                n_col = [0]
                for n in range(4):
                    n_col[0] = n // 2
                    if n < 2:
                        sp.dma_start(fw[n][:, :, :], agg_view[n, :, :, 0:BANK]).then_inc(fw_loaded[n], 16)
                    else:
                        fw_load(agg_view, n, n - 2, n)
                sp.wait_ge(thought_ready, 2)
                sp.dma_start(bias_rows[:, :], d2_b.partition_broadcast(B)).then_inc(bias_loaded, 16)

                def start(b):
                    for t in range(TB):
                        if t < 2:
                            sp.wait_ge(x_turned, after(TB * b))
                        else:
                            sp.wait_ge(x_turned, after(TB * b + t - 1))
                        sp.dma_start(xn[t % 2][:, :], x[b, bass.ts(t, P), :]).then_inc(x_loaded[t % 2], 16)
                    sp.wait_ge(k_full, 4 * b + 4)
                    for s in range(2):
                        sp.dma_start(w[:, s, :].bitcast(F32), WT[s, :, :]).then_inc(w_loaded[s], 16)

                def body(b, layer, j, g, it):
                    def load(tile):
                        s = tile % 2
                        count = FW_FIRST + FW_TILES * it + tile
                        sp.wait_ge(fw_used, count - 1)
                        if layer == 0:
                            src = d1_view[tile % 2, :, :, bass.ts(4 * j + tile // 2, BANK)]
                        else:
                            src = d2_view[tile, :, :, bass.ts(j, BANK)]
                        sp.dma_start(fw[s][:, :, :], src).then_inc(fw_loaded[s], 16)

                    load(0)
                    load(1)
                    sp.wait_ge(q_full, 4 * it + 2)
                    sp.dma_start(w[:, 0, :].bitcast(F32), WT[2 * g + 2, :, :]).then_inc(w_loaded[0], 16)
                    for u in range(UNITS + 4):
                        if u == 16:
                            sp.wait_ge(q_full, 4 * it + 4)
                            sp.dma_start(w[:, 1, :].bitcast(F32), WT[2 * g + 3, :, :]).then_inc(w_loaded[1], 16)
                        tile = ffn_tile(layer, u)
                        if tile is not None and tile + 2 < FW_TILES:
                            load(tile + 2)
                        if u >= 5 and u % 2 == 1:
                            n = (u - 5) // 2
                            pair, qb = n // TB, n % TB
                            sp.wait_ge(y_ready, after(2 * TB * it + n + 1))
                            sp.dma_start(Y[b, bass.ts(qb, P), bass.ts(2 * g + pair, P)],
                                         y[n % 2][:, :, :].rearrange("p h d -> p (h d)")).then_inc(
                                y_stored[n % 2], 16)

                loops(sp, start, nothing, nothing, body)
                sp.wait_ge(thought_ready, 2 + 2 * B)
                sp.dma_start(bias_rows[:, :], bc_b.partition_broadcast(B)).then_inc(bias_loaded, 16)
                for n in range(4):
                    n_col[0] = n // 2
                    fw_load(bc_view, n, n % 2, FW_FIRST + FW_TILES * 4 * B + n)
                sp.wait_ge(thought_ready, 4 + 2 * B)
                sp.dma_start(BC[:, :], t_rows[:, :]).then_inc(bc_stored, 16)
                sp.wait_ge(bc_stored, 16)
                for n in range(2):
                    sp.wait_ge(y_stored[n], landed(TB * 4 * B))
                for s in range(2):
                    sp.wait_ge(w_loaded[s], 16 * (1 + 5 * B))

            @block.gpsimd
            def _(pool):
                pool.memset(ffn_rows[:, :], 0.0).then_inc(rows_zeroed, 1)
                pool.memset(ident[:, :], 0.0)
                pool.memset(mask[:, :], 0.0)
                pool.memset(mask4[:, :], 0.0)
                pool.memset(cols[:, :, :], 0.0)
                pool.memset(v[:, :, :, HS:HS + 1], 1.0)
                pool.memset(eps_x[:, :], EPS_X)
                pool.memset(eps_ffn[:, :], EPS_FFN)
                pool.memset(minus_half[:, :], -0.5).then_inc(filled, 1)
                pool.wait_ge(filled, 1)
                pool.affine_select(out=ident[:, :], in_=ident[:, :], compare_op=ALU.not_equal, fill=1.0,
                                   base=0, pattern=[[-1, P]], channel_multiplier=1).then_inc(ident_ready, 1)
                for m in (mask, mask4):
                    pool.affine_select(out=m[:, 0:P], in_=m[:, 0:P], compare_op=ALU.is_ge, fill=NEG,
                                       base=-1, pattern=[[1, P]], channel_multiplier=-1)
                    pool.affine_select(out=m[:, WB * P:WIDE], in_=m[:, WB * P:WIDE], compare_op=ALU.is_ge, fill=NEG,
                                       base=0, pattern=[[-1, P]], channel_multiplier=1).then_inc(masks_ready, 1)
                pool.wait_ge(masks_ready, 2)
                pool.memset(mask4[:, 0:SINK], 0.0).then_inc(masks_ready, 1)

                ln_rstd(pool, ln, 0, mv[0], rstd[0], B, eps_x, minus_half)
                ln_rstd(pool, ln, 1, mv[1], rstd[1], B, eps_ffn, minus_half)

                def start(b):
                    for t in range(TB):
                        ln_rstd(pool, ln, Q_LNS + LNS * b + t, mv[t % 2], rstd[t % 2], P, eps_x, minus_half)
                    ln_rstd(pool, ln, Q_LNS + LNS * b + TB, mv[0], rstd[0], B, eps_ffn, minus_half)

                with pool.Fori(0, B) as b:
                    start(b)

            @block.scalar
            def _(act):
                def copy_rows(tiles):
                    act.wait_ge(fw_used, tiles)
                    act.activation(rows[:, :], j_ps[:, :], ACT.Copy).then_inc(rows_ready, 1)

                for c in range(2):
                    copy_rows(2 * c + 2)

                def start(b):
                    for t in range(TB + 1):
                        if t < TB:
                            act.wait_ge(x_turned, after(TB * b + t + 1))
                            act.activation(x_hi[:, :, bass.ts(t, P)],
                                           s_ps[t % 2][:, :].rearrange("p (k n) -> p k n", n=P),
                                           ACT.Copy).then_inc(x_hi_ready, 1)
                        if t >= 1:
                            act.wait_ge(v_full, TB * b + t)
                            o = BANK * ((t - 1) % 2)
                            act.activation(v[:, t - 1, :, 0:HS],
                                           t_ps[:, o:o + KV * HS].rearrange("p (g d) -> p g d", d=HS),
                                           ACT.Copy).then_inc(v_ready, 1)
                        for n in {5: (0, 1), TB - 1: (2, 3)}.get(t, ()):
                            k_copies(b, n)

                def k_copies(b, n):
                    m, ch = n % 2, n // 2
                    src = (j_ps, o_ps)[n % 2]
                    act.wait_ge(k_full, 4 * b + n + 1)
                    for head in range(2):
                        for half in range(2):
                            last = act.activation(k_hi[HS * half:HS * half + HS, 2 * m + head, bass.ts(ch, BANK)],
                                                  src[HS * head:HS * head + HS, :], ACT.Copy)
                    last.then_inc(k_hi_ready, 1)

                def q_copies(it, n):
                    pair, ch = n // 2, n % 2
                    src = s_ps[0][:, bass.ts(n, BANK)] if n < 2 else j_ps
                    act.wait_ge(q_full, 4 * it + n + 1)
                    for head in range(2):
                        h = slice(HS * head, HS * head + HS)
                        last = act.activation(q[2 * pair + head][h, bass.ts(ch, BANK)], src[h, 0:BANK], ACT.Copy)
                    last.then_inc(q_hi_ready, 1)

                def output_start(b):
                    act.wait_ge(hid_ready, after(8 * b + 8))
                    act.activation(cols[:, :, 0:B], h_pre[:, :, :], ACT.Gelu).then_inc(gelu_done, 1)

                def body(b, layer, j, g, it):
                    q_copies(it, 0)
                    q_copies(it, 1)
                    for s in range(UNITS + 3):
                        if 2 <= s < UNITS + 2:
                            u = s - 2
                            n = min(blocks_of(unit(u)[1]), WB) * P
                            act.wait_ge(turned, UNITS * it + u + 1)
                            act.activation(probs_t[u % 2][:, 0:n], t_ps[:, 0:n], ACT.Copy).then_inc(copied_a, 1)
                        if s < UNITS:
                            _, qb, _ = unit(s)
                            n = blocks_of(qb) * P + (SINK if qb > WB else 0)
                            act.wait_ge(masked, UNITS * it + s + 1)
                            act.activation(probs[s % 3][:, 0:n], probs[s % 3][:, 0:n], ACT.Exp,
                                           bias=neg_max[:, s % 4:s % 4 + 1], scale=-1.0).then_inc(exp_done, 1)
                        if s == 7:
                            q_copies(it, 2)
                        if s == 15:
                            q_copies(it, 3)
                        if layer == 0 and s >= 16 and s < UNITS and s % 4 == 1:
                            n = (s - 16) // 4
                            copy_rows(FW_FIRST + FW_TILES * it + 2 * n + 2)
                        if layer == 1 and s == UNITS:
                            copy_rows(FW_FIRST + FW_TILES * (it + 1))

                loops(act, start, nothing, output_start, body)
                for c in range(2):
                    copy_rows(FW_FIRST + FW_TILES * 4 * B + 2 * c + 2)

            @block.tensor
            def _(pe):
                start_counted(pe, x_turned)
                pe.wait_ge(ident_ready, 1)
                pe.wait_ge(fold_ready, 1)

                def turn_rows(p):
                    for k in range(KB):
                        last = pe.matmul(f_cols[:, B * k:B * k + B], ffn_rows[0:64, bass.ts(k, P)], ident[0:64, p:p + B],
                                         start=True, stop=True)
                    last.then_inc(f_turned, 1)

                def ffn_products(cols, first, tile, count, start, stop):
                    s = tile % 2
                    pe.wait_ge(fw_loaded[s], 16 * (count // 2) + 16)
                    for k in range(FW_BLOCKS):
                        last = pe.matmul(j_ps[32 * k:32 * k + 32, :], cols[:, first + k, :], fw[s][:, k, :],
                                         start=start, stop=stop)
                    last.then_inc(fw_used, 1)

                def fold_rows(chunk):
                    pe.wait_ge(rows_ready, chunk + 1)
                    pe.matmul(j_ps[0:B, :], fold[:, :], rows[:, :], start=True, stop=True).then_inc(folded, 1)

                pe.wait_ge(t_rows_ready, 1)
                turn_rows(32)
                pe.wait_ge(cols_ready, 1)

                def small_product(cols, tiles_before, chunks_before_, thoughts_before):
                    for c in range(2):
                        if c == 1:
                            pe.wait_ge(thought_ready, thoughts_before + 1)
                        for half in range(2):
                            ffn_products(cols, FW_BLOCKS * half, half, tiles_before + 2 * c + half,
                                         half == 0, half == 1)
                        fold_rows(chunks_before_ + c)

                small_product(cols, 0, 0, 0)

                def proj(out, wslot, ch):
                    steps = []
                    for c in range(KB):
                        for wp, xs in ((0, x_hi), (0, x_lo), (1, x_hi)):
                            steps.append((w[:, wslot, wp * C + c * P:wp * C + c * P + P], xs[:, c, bass.ts(ch, BANK)],
                                          c == 0 and wp == 0 and xs is x_hi, c == KB - 1 and wp == 1))

                    def run(a, z):
                        last = None
                        for lhs, rhs, first, final in steps[a:z]:
                            last = pe.matmul(out, lhs, rhs, start=first, stop=final)
                        return last
                    return run

                STEPS = 3 * KB

                def start(b):
                    def turn(t):
                        pe.wait_ge(xn_ready, TB * b + t + 1)
                        if t >= 2:
                            pe.wait_ge(x_lo_ready, TB * b + t - 1)
                        for c in range(KB):
                            last = pe.transpose(s_ps[t % 2][:, bass.ts(c, P)], xn[t % 2][:, bass.ts(c, P)], ident[:, :])
                        last.then_inc(x_turned, 1)

                    def v_proj(t):
                        pe.wait_ge(x_lo_ready, TB * b + t + 1)
                        if t == 0:
                            for s in (2, 3):
                                pe.wait_ge(w_loaded[s], 16)
                        if t >= 2:
                            pe.wait_ge(v_ready, TB * b + t - 1)
                        o = BANK * (t % 2)
                        for c in range(KB):
                            for xs, wp in ((x_hi, 0), (x_hi, 1), (x_lo, 0)):
                                last = pe.matmul(t_ps[:, o:o + KV * HS], xs[:, c, bass.ts(t, P)],
                                                 w[:, 2:4, wp * C + c * P:wp * C + c * P + P],
                                                 start=(c == 0 and xs is x_hi and wp == 0),
                                                 stop=(c == KB - 1 and xs is x_lo))
                        last.then_inc(v_full, 1)

                    def k_proj(n):
                        if n < 2:
                            pe.wait_ge(w_loaded[n], 16 * (5 * b) + 16)
                        if n == 0:
                            pe.wait_ge(thought_ready, 2 + 2 * b)
                        if n >= 2:
                            pe.wait_ge(k_lo_ready, 4 * b + n - 1)
                        out = (j_ps, o_ps)[n % 2]
                        proj(out[:, :], n % 2, n // 2)(0, STEPS).then_inc(k_full, 1)

                    for t in range(TB + 1):
                        if t < TB:
                            turn(t)
                        if t == TB:
                            pe.wait_ge(x_lo_ready, TB * b + TB)
                            k_proj(2)
                            k_proj(3)
                        if t >= 1:
                            v_proj(t - 1)
                        if t == 5:
                            k_proj(0)
                            k_proj(1)

                def hidden_start(b):
                    pe.wait_ge(t_rows_ready, 2 + b)
                    pe.wait_ge(k_lo_ready, 4 * b + 3)
                    turn_rows(32)

                def body(b, layer, j, g, it):
                    pe.wait_ge(w_loaded[0], 16 * (5 * b + g) + 32)
                    for ch in range(2):
                        proj(s_ps[0][:, bass.ts(ch, BANK)], 0, ch)(0, STEPS).then_inc(q_full, 1)
                    q_b = [proj(j_ps[:, :], 1, ch) for ch in range(2)]

                    def scores(u):
                        pair, qb, head = unit(u)
                        if u % 16 == 0:
                            pe.wait_ge(q_lo_ready, 4 * it + (2 if u == 0 else 4))
                        if u >= 2:
                            pe.wait_ge(masked, UNITS * it + u - 1)
                        n = blocks_of(qb)
                        lhs = q[2 * pair + head][:, bass.ts(qb, P)]
                        first = (qb - n + 1) * P
                        pieces = [(0, first, min(n, WB) * P)]
                        if n > WB:
                            pieces.append((BANK, first + BANK, P))
                        if qb > WB:
                            pieces.append((WIDE, 0, SINK))
                        for o, key, width in pieces:
                            for part, k in enumerate((k_hi, k_lo)):
                                last = pe.matmul(s_ps[u % 2][:, o:o + width], lhs, k[:, g, key:key + width],
                                                 start=part == 0, stop=part == 1)
                        last.then_inc(scores_ready, 1)

                    def turn_probs(u):
                        _, qb, _ = unit(u)
                        pe.wait_ge(exp_done, UNITS * it + u + 1)
                        if u == 0 and layer == 0:
                            pe.wait_ge(v_ready, TB * b + TB)
                        if u >= 1:
                            pe.wait_ge(copied_a, UNITS * it + u)
                        if wide[u] > 0:
                            pe.wait_ge(copied_b, wide[UNITS] * it + wide[u])
                        n = blocks_of(qb)
                        for i in range(n):
                            last = pe.transpose(t_ps[:, bass.ts(i, P)], probs[u % 3][:, bass.ts(i, P)], ident[:, :])
                        if qb > WB:
                            last = pe.transpose(t_ps[0:SINK, WIDE:WIDE + P], probs[u % 3][:, WIDE:WIDE + SINK],
                                                ident[:, :])
                        last.then_inc(turned, 1)

                    def values(u):
                        _, qb, head = unit(u)
                        n = blocks_of(qb)
                        block_no = u // 2
                        pe.wait_ge(copied_a, UNITS * it + u + 1)
                        if n > WB:
                            pe.wait_ge(copied_b, wide[UNITS] * it + wide[u + 1])
                        if u == 0 and layer == 0:
                            pe.wait_ge(k_lo_ready, 4 * b + 4)
                        if head == 0:
                            pe.wait_ge(y_ready, after(2 * TB * it + block_no))
                        out = o_view[:, head, :]
                        for i in range(n):
                            last = pe.matmul(out, probs_t[u % 2][:, bass.ts(i, P)], v[:, qb - n + 1 + i, g, :],
                                             start=i == 0, stop=(i == n - 1 and qb <= WB))
                        if qb > WB:
                            last = pe.matmul(out, probs_t[u % 2][0:SINK, WIDE:WIDE + P], v[0:SINK, 0, g, :],
                                             start=False, stop=True)
                        last.then_inc(pv_done, 1)

                    def ffn(u):
                        tile = ffn_tile(layer, u)
                        if tile is not None:
                            count = FW_FIRST + FW_TILES * it + tile
                            if layer == 0:
                                if tile % 2 == 0 and tile:
                                    pe.wait_ge(hid_ready, after(8 * b + 4 * j + tile // 2))
                                ffn_products(cols, FW_BLOCKS * (tile % 2), tile, count, tile % 2 == 0, tile % 2 == 1)
                            else:
                                if u == 17:
                                    pe.wait_ge(gelu_done, b + 1)
                                ffn_products(cols, FW_BLOCKS * tile, tile, count, tile == 0, tile == FW_TILES - 1)
                        if layer == 0 and u >= 16 and u % 4 == 3:
                            n = (u - 16) // 4
                            pe.wait_ge(rows_ready, chunks_before(b, layer, j) + n + 1)
                            for i in range(4):
                                last = pe.matmul(f_hid[:, i, :], rows[:, bass.ts(i, P)], fold[:, :],
                                                 start=True, stop=True)
                            last.then_inc(hid_turned, 1)

                    for s in range(UNITS + 3):
                        if s < UNITS:
                            scores(s)
                        if 2 <= s < UNITS + 2:
                            turn_probs(s - 2)
                        if s < 16:
                            if s == 0:
                                pe.wait_ge(w_loaded[1], 16 * (5 * b + g) + 32)
                                if layer == 0:
                                    pe.wait_ge(cols_ready, 2 + b)
                                    pe.wait_ge(hid_ready, after(8 * b + 4 * j))
                                else:
                                    pe.wait_ge(hid_ready, after(8 * b + 8))
                                    pe.wait_ge(thought_ready, 2 + 2 * b + j)
                            if s == 8:
                                pe.wait_ge(q_lo_ready, 4 * it + 3)
                            ch, i = s // 8, s % 8
                            if i < 7:
                                cuts = [0, 4, 8, 12, 15, 18, 21, 24]
                                last = q_b[ch](cuts[i], cuts[i + 1])
                                if i == 6:
                                    last.then_inc(q_full, 1)
                        elif s < UNITS:
                            ffn(s)
                        if s >= 3:
                            values(s - 3)
                    if layer == 1:
                        fold_rows(chunks_before(b, layer, j))

                loops(pe, start, hidden_start, nothing, body)
                pe.wait_ge(thought_ready, 2 + 2 * B)
                turn_rows(0)
                pe.wait_ge(cols_ready, 2 + B)
                small_product(cols, FW_FIRST + FW_TILES * 4 * B, 2 + 10 * B, 2 + 2 * B)

            @block.vector
            def _(dve):
                start_counted(dve, y_ready, hid_ready)
                dve.wait_ge(ident_ready, 1)
                dve.tensor_reduce(fold[:, :], ident[:, :].rearrange("p (j n) -> p n j", j=4)[:, 0:B, :], AX.X,
                                  ALU.add).then_inc(fold_ready, 1)

                def scale_cols(gamma, turns):
                    dve.wait_ge(f_turned, turns + 1)
                    for k in range(KB):
                        last = dve.tensor_scalar(cols[:, k, 0:B], f_cols[:, B * k:B * k + B],
                                                 affine[:, gamma, k:k + 1], affine[:, gamma + 1, k:k + 1],
                                                 ALU.mult, ALU.add)
                    last.then_inc(cols_ready, 1)

                def add_rows(c, count, dst, carry):
                    part = bass.ts(c, BANK)
                    dve.wait_ge(folded, count + 1)
                    if carry is None:
                        dve.tensor_tensor(dst[:, part], j_ps[0:B, :], bias_rows[:, part],
                                          ALU.add).then_inc(thought_ready, 1)
                    else:
                        dve.tensor_tensor(rows[0:B, :], j_ps[0:B, :], bias_rows[:, part],
                                          ALU.add).then_inc(biased, 1)
                        dve.wait_ge(biased, count - 1)
                        dve.tensor_tensor(dst[:, part], carry[:, part], rows[0:B, :],
                                          ALU.add).then_inc(thought_ready, 1)

                dve.wait_ge(last_loaded, 16)
                ln_statistics(dve, ln, 0, thought, B, st[0], mv[0])
                ln_apply(dve, ln, 0, thought[:, :], thought[:, :], mv[0], rstd[0], B).then_inc(last_normed, 1)
                dve.wait_ge(last_normed, 1)
                ln_statistics(dve, ln, 1, thought, B, st[1], mv[1])
                ln_apply(dve, ln, 1, t_rows[:, :], thought[:, :], mv[1], rstd[1], B).then_inc(t_rows_ready, 1)
                dve.wait_ge(small_loaded, 16 * 5)
                dve.wait_ge(filled, 1)
                scale_cols(0, 0)
                dve.wait_ge(bias_loaded, 16)
                for c in range(2):
                    add_rows(c, c, thought, None)
                dve.wait_ge(bias_loaded, 32)

                def start(b):
                    def stats(t):
                        dve.wait_ge(x_loaded[t % 2], 16 * (4 * b + t // 2) + 16)
                        ln_statistics(dve, ln, Q_LNS + LNS * b + t, xn[t % 2], P, st[t % 2], mv[t % 2])

                    def x_low(t):
                        dve.wait_ge(x_hi_ready, TB * b + t + 1)
                        dve.tensor_tensor(x_lo[:, :, bass.ts(t, P)],
                                          s_ps[t % 2][:, :].rearrange("p (k n) -> p k n", n=P),
                                          x_hi[:, :, bass.ts(t, P)].bitcast(F32), ALU.subtract).then_inc(x_lo_ready, 1)

                    stats(0)
                    for t in range(TB + 1):
                        if t < TB:
                            ln_apply(dve, ln, Q_LNS + LNS * b + t, xn[t % 2][:, :], xn[t % 2][:, :], mv[t % 2],
                                     rstd[t % 2], P).then_inc(xn_ready, 1)
                        if t >= 1:
                            x_low(t - 1)
                        if t + 1 < TB:
                            stats(t + 1)
                        if t == 6:
                            k_low(b, 0)
                            k_low(b, 1)
                    n = Q_LNS + LNS * b + TB
                    dve.wait_ge(thought_ready, 2 + 2 * b)
                    ln_statistics(dve, ln, n, thought, B, st[0], mv[0])
                    ln_apply(dve, ln, n, t_rows[:, :], thought[:, :], mv[0], rstd[0], B).then_inc(t_rows_ready, 1)
                    k_low(b, 2)
                    k_low(b, 3)

                def k_low(b, n):
                    m, ch = n % 2, n // 2
                    src = (j_ps, o_ps)[n % 2]
                    dve.wait_ge(k_hi_ready, 4 * b + n + 1)
                    for head in range(2):
                        h = slice(HS * head, HS * head + HS)
                        for half in range(2):
                            last = dve.tensor_tensor(k_lo[HS * half:HS * half + HS, 2 * m + head, bass.ts(ch, BANK)],
                                                     src[h, :], k_hi[h, 2 * m + head, bass.ts(ch, BANK)].bitcast(F32),
                                                     ALU.subtract)
                    last.then_inc(k_lo_ready, 1)

                def q_low(it, n):
                    pair, ch = n // 2, n % 2
                    src = s_ps[0][:, bass.ts(n, BANK)] if n < 2 else j_ps
                    dve.wait_ge(q_hi_ready, 4 * it + n + 1)
                    for head in range(2):
                        hi = slice(HS * head, HS * head + HS)
                        lo = slice(HS * (1 - head), HS * (1 - head) + HS)
                        last = dve.tensor_tensor(q[2 * pair + head][lo, bass.ts(ch, BANK)], src[hi, 0:BANK],
                                                 q[2 * pair + head][hi, bass.ts(ch, BANK)].bitcast(F32), ALU.subtract)
                    last.then_inc(q_lo_ready, 1)

                def hidden_start(b):
                    scale_cols(2, 1 + b)

                def body(b, layer, j, g, it):
                    q_low(it, 0)
                    q_low(it, 1)
                    for s in range(UNITS + 4):
                        if s >= 5 and s % 2 == 1:
                            n = (s - 5) // 2
                            slot = n % 2
                            dve.wait_ge(pv_done, UNITS * it + 2 * n + 2)
                            dve.reciprocal(inv_sum[:, slot, :], o_view[:, :, HS]).then_inc(inv_ready, 1)
                            dve.wait_ge(inv_ready, 2 * TB * it + n + 1)
                            dve.wait_ge(y_stored[n % 2], landed(TB * it + n // 2))
                            for head in range(2):
                                last = dve.tensor_scalar(y[n % 2][:, head, :], o_view[:, head, 0:HS],
                                                         inv_sum[:, slot, head:head + 1], None, ALU.mult)
                            last.then_inc(y_ready, 1)
                        if s < UNITS:
                            _, qb, _ = unit(s)
                            n = blocks_of(qb) * P
                            if qb == WB:
                                m, hidden = mask4[:, 0:n], 0
                            else:
                                m = mask[:, WIDE - n:WIDE + (SINK if qb > WB else 0)]
                            width = n + (SINK if qb > WB else 0)
                            if s == 0:
                                dve.wait_ge(masks_ready, 3)
                            dve.wait_ge(scores_ready, UNITS * it + s + 1)
                            dve.sem_inc(wait_over, 1)
                            dve.tensor_tensor_reduce(out=probs[s % 3][:, 0:width], in0=s_ps[s % 2][:, 0:width], in1=m,
                                                     scale=-SCALE, scalar=-NEG, op0=ALU.add, op1=ALU.min,
                                                     accum_out=neg_max[:, s % 4:s % 4 + 1]).then_inc(masked, 1)
                        if 2 <= s < UNITS + 2 and blocks_of(unit(s - 2)[1]) > WB:
                            u = s - 2
                            dve.wait_ge(turned, UNITS * it + u + 1)
                            last = dve.tensor_copy(probs_t[u % 2][:, WB * P:WIDE], t_ps[:, WB * P:WIDE])
                            if unit(u)[1] > WB:
                                last = dve.tensor_copy(probs_t[u % 2][0:SINK, WIDE:WIDE + P],
                                                       t_ps[0:SINK, WIDE:WIDE + P])
                            last.then_inc(copied_b, 1)
                        if s == 7:
                            q_low(it, 2)
                        if s == 15:
                            q_low(it, 3)
                        if layer == 0 and 16 <= s < UNITS and s % 4 == 3:
                            n = (s - 16) // 4
                            dve.wait_ge(hid_turned, 8 * b + 4 * j + n + 1)
                            for row in range(B):
                                last = dve.tensor_tensor(h_pre[:, bass.ds(16 * j + 4 * n, 4), row], f_hid[:, :, row],
                                                         d1_bias[:, bass.ds(16 * j + 4 * n, 4)], ALU.add)
                            last.then_inc(hid_ready, 1)
                    if layer == 1:
                        add_rows(j, 2 + 2 * b + j, thought, thought)

                loops(dve, start, hidden_start, nothing, body)
                dve.wait_ge(f_turned, 2 + B)
                dve.tensor_copy(cols[:, 0:KB, 0:B], f_cols.rearrange("p (k b) -> p k b", b=B)).then_inc(cols_ready, 1)
                dve.wait_ge(bias_loaded, 48)
                for c in range(2):
                    add_rows(c, 2 + 2 * B + c, t_rows, None)


def finish(nc, WT, Y, BC, x, gate_w, gate_b, out_gamma, out_beta, out):
    TILES = B * TB
    with ExitStack() as ctx:
        def sb(name, shape, dt=F32):
            return ctx.enter_context(nc.sbuf_tensor(name, shape, dt))

        def ps(name):
            return ctx.enter_context(nc.psum_tensor(name, [P, C], F32))

        def sem(name):
            return ctx.enter_context(nc.semaphore(name))

        wo = sb("wo", [P, O_TILES, 2, KB, P], F32R)
        g_hi, g_lo = sb("g_hi", [P, KB, C], F32R), sb("g_lo", [P, KB, C], F32R)
        gate_bias, gamma, beta, bc = (sb(n, [P, C]) for n in ("gate_bias", "gamma", "beta", "bc"))
        xt = [sb(f"b_x{s}", [P, C]) for s in range(2)]
        xn = [sb(f"b_xn{s}", [P, C]) for s in range(2)]
        yt = [sb(f"b_y{s}", [P, C]) for s in range(2)]
        x_hi, x_lo, y_hi, y_lo = (sb(n, [P, KB, P], F32R) for n in ("bx_hi", "bx_lo", "by_hi", "by_lo"))
        a, c_, res = sb("b_a", [P, C]), sb("b_c", [P, C]), sb("b_res", [P, C])
        ident = sb("b_ident", [P, P])
        eps_x, eps_ffn, minus_half = sb("b_eps_x", [P, 1]), sb("b_eps_ffn", [P, 1]), sb("b_minus_half", [P, 1])
        st = [sb(f"b_st{s}", [P, 2, 6]) for s in range(2)]
        mv = [sb(f"b_mv{s}", [P, 2]) for s in range(2)]
        rstd = [sb(f"b_rstd{s}", [P, 2]) for s in range(2)]
        x_ps, y_ps, gate_ps, out_ps = ps("x_ps"), ps("y_ps"), ps("gate_ps"), ps("out_ps")

        vec_loaded, wo_loaded = sem("b_vec_loaded"), sem("b_wo_loaded")
        raw_loaded = [sem(f"b_raw_loaded{s}") for s in range(2)]
        bc_loaded = sem("b_bc_loaded")
        x_loaded = [sem(f"b_x_loaded{s}") for s in range(2)]
        y_loaded = [sem(f"b_y_loaded{s}") for s in range(2)]
        stored = sem("b_stored")
        filled, ident_ready, gw_hi, gw_lo = sem("b_filled"), sem("b_ident_ready"), sem("b_gw_hi"), sem("b_gw_lo")
        ln = LayerNormStats(sem("b_ln_stats"), sem("b_ln_var"), sem("b_ln_rstd"), sem("b_ln_eps"), sem("b_ln_wait_over"))
        xn_ready, turned, hi_ready, lo_ready = sem("b_xn_ready"), sem("b_turned"), sem("b_hi"), sem("b_lo")
        gate_done, out_done = sem("b_gate_done"), sem("b_out_done")
        z_ready, sig_ready, mixed, added = sem("b_z"), sem("b_sig"), sem("b_mixed"), sem("b_added")
        normed, scaled, shifted, sig2_ready = sem("b_normed"), sem("b_scaled"), sem("b_shifted"), sem("b_sig2")
        silu_done, gated, res_ready = sem("b_silu"), sem("b_gated"), sem("b_res_ready")

        def pre(t):
            return 2 * t

        def pre_no(t):
            return t if isinstance(t, int) and t < 2 else 2 * t - 2

        def post_no(t):
            return 2 * t + 2 if not isinstance(t, int) or t <= TILES - 2 else 2 * TILES - 1

        x_flat = x.rearrange("b t c -> (b t) c")
        y_flat = Y.rearrange("b t c -> (b t) c")
        out_flat = out.rearrange("b t c -> (b t) c")

        def tiles(eng, body):
            for b in range(B):
                pairs = TB // 2 - (b == B - 1)
                with eng.Fori(0, pairs) as i:
                    for s in range(2):
                        body(TB * b + 2 * i + s, s, b, s == 0 and "i", i)
            for s in range(2):
                body(TILES - 2 + s, s, B - 1, False, None)

        with nc.Block() as block:
            @block.sync
            def _(sp):
                start_counted(sp, stored, dma=True)
                for n, (dst, vec) in enumerate(((gate_bias, gate_b), (gamma, out_gamma), (beta, out_beta))):
                    sp.dma_start(dst[:, :], vec.partition_broadcast(P)).then_inc(vec_loaded, 16)
                for s in range(2):
                    sp.dma_start(xt[s][:, :], x_flat[bass.ts(s, P), :]).then_inc(x_loaded[s], 16)
                for c in range(KB):
                    if c >= 2:
                        sp.wait_ge(gw_lo, c - 1)
                    sp.dma_start(yt[c % 2][:, :], gate_w[bass.ts(c, P), :]).then_inc(raw_loaded[c % 2], 16)
                for n in range(O_TILES):
                    sp.dma_start(wo[:, n].rearrange("p a k m -> p (a k m)").bitcast(F32), WT[O0 + n, :, :]).then_inc(wo_loaded, 16)
                sp.wait_ge(gw_lo, KB)
                for s in range(2):
                    sp.dma_start(yt[s][:, :], y_flat[bass.ts(s, P), :]).then_inc(y_loaded[s], 16)

                def load_bc(b):
                    if b:
                        sp.wait_ge(mixed, TB * b)
                    sp.dma_start(bc[:, :], BC[b, :].partition_broadcast(P)).then_inc(bc_loaded, 16)

                def body(t, s, b, _, i):
                    more = not isinstance(t, int)
                    if more:
                        sp.wait_ge(turned, t + 1)
                        sp.dma_start(yt[s][:, :], y_flat[bass.ds(P * (t + 2), P), :]).then_inc(y_loaded[s], 16)
                    sp.wait_ge(res_ready, after(t + 1))
                    sp.dma_start(out_flat[bass.ts(t, P), :], res[:, :]).then_inc(stored, 16)
                    if more:
                        sp.dma_start(xt[s][:, :], x_flat[bass.ds(P * (t + 2), P), :]).then_inc(x_loaded[s], 16)

                for b in range(B):
                    load_bc(b)
                    with sp.Fori(0, TB // 2 - (b == B - 1)) as i:
                        for s in range(2):
                            body(TB * b + 2 * i + s, s, b, None, i)
                for s in range(2):
                    body(TILES - 2 + s, s, B - 1, None, None)
                sp.wait_ge(stored, landed(TILES))

            @block.gpsimd
            def _(pool):
                pool.memset(ident[:, :], 0.0)
                pool.memset(eps_x[:, :], EPS_X)
                pool.memset(eps_ffn[:, :], EPS_FFN)
                pool.memset(minus_half[:, :], -0.5).then_inc(filled, 1)
                pool.wait_ge(filled, 1)
                pool.affine_select(out=ident[:, :], in_=ident[:, :], compare_op=ALU.not_equal, fill=1.0,
                                   base=0, pattern=[[-1, P]], channel_multiplier=1).then_inc(ident_ready, 1)
                for s in range(2):
                    ln_rstd(pool, ln, s, mv[s], rstd[s], P, eps_x, minus_half)

                def body(t, s, b, _, i):
                    ln_rstd(pool, ln, post_no(t), mv[s], rstd[s], P, eps_ffn, minus_half)
                    if not isinstance(t, int):
                        ln_rstd(pool, ln, post_no(t) + 1, mv[s], rstd[s], P, eps_x, minus_half)
                tiles(pool, body)

            @block.scalar
            def _(act):
                for c in range(KB):
                    act.wait_ge(raw_loaded[c % 2], 16 * (c // 2) + 16)
                    act.activation(g_hi[:, c, :], yt[c % 2][:, :], ACT.Copy).then_inc(gw_hi, 1)

                def hi_parts(n):
                    act.wait_ge(turned, n + 1)
                    for dst, src in ((x_hi, x_ps), (y_hi, y_ps)):
                        last = act.activation(dst[:, :, :].rearrange("p k n -> p (k n)"), src[:, :], ACT.Copy)
                    last.then_inc(hi_ready, 1)

                hi_parts(0)

                def body(t, s, b, _, i):
                    last_block = isinstance(t, int) and t == TILES - 1
                    act.wait_ge(z_ready, t + 1)
                    act.activation(a[:, :], a[:, :], ACT.Sigmoid).then_inc(sig_ready, 1)
                    if not last_block:
                        act.wait_ge(out_done, t + 1)
                        hi_parts(t + 1)
                    act.wait_ge(shifted, t + 1)
                    act.activation(c_[:, :], a[:, :], ACT.Sigmoid).then_inc(sig2_ready, 1)
                tiles(act, body)

            @block.tensor
            def _(pe):
                pe.wait_ge(ident_ready, 1)

                def turn(t, s, count16):
                    pe.wait_ge(xn_ready, t + 1)
                    pe.wait_ge(y_loaded[s], count16)
                    for c in range(KB):
                        pe.transpose(x_ps[:, bass.ts(c, P)], xn[s][:, bass.ts(c, P)], ident[:, :])
                    for c in range(KB):
                        last = pe.transpose(y_ps[:, bass.ts(c, P)], yt[s][:, bass.ts(c, P)], ident[:, :])
                    last.then_inc(turned, 1)

                def products(out_, hi, lo, w_hi, w_lo):
                    for c in range(KB):
                        for lhs, rhs in ((hi, w_hi), (hi, w_lo), (lo, w_hi)):
                            for half in range(2):
                                last = pe.matmul(out_[:, bass.ts(half, BANK)], lhs[:, c, :], rhs(c, half),
                                                 start=(c == 0 and lhs is hi and rhs is w_hi),
                                                 stop=(c == KB - 1 and lhs is lo))
                    return last

                def gate_part(part):
                    return lambda c, half: part[:, c, bass.ts(half, BANK)]

                def wo_part(part):
                    return lambda c, half: wo[:, 4 * half:4 * half + 4, part, c, :]

                parts = [gate_part(g_hi), gate_part(g_lo), wo_part(0), wo_part(1)]
                turn(0, 0, 16)
                pe.wait_ge(gw_lo, KB)
                pe.wait_ge(wo_loaded, 16 * O_TILES)

                def body(t, s, b, _, i):
                    last_block = isinstance(t, int) and t == TILES - 1
                    pe.wait_ge(lo_ready, t + 1)
                    products(gate_ps, x_hi, x_lo, parts[0], parts[1]).then_inc(gate_done, 1)
                    if not last_block:
                        half = (TB // 2) * b
                        nxt = (half + i if i is not None else TILES // 2 - 1) + (s == 1)
                        turn(t + 1, 1 - s, 16 * nxt + 16)
                    pe.wait_ge(gated, after(t))
                    products(out_ps, y_hi, y_lo, parts[2], parts[3]).then_inc(out_done, 1)
                tiles(pe, body)

            @block.vector
            def _(dve):
                start_counted(dve, res_ready, gated)
                for c in range(KB):
                    dve.wait_ge(gw_hi, c + 1)
                    dve.tensor_tensor(g_lo[:, c, :], yt[c % 2][:, :], g_hi[:, c, :].bitcast(F32),
                                      ALU.subtract).then_inc(gw_lo, 1)

                def norm_input(n, s, loads):
                    dve.wait_ge(x_loaded[s], 16 * loads)
                    ln_statistics(dve, ln, n, xt[s], P, st[s], mv[s])
                    ln_apply(dve, ln, n, xn[s][:, :], xt[s][:, :], mv[s], rstd[s], P).then_inc(xn_ready, 1)

                def lo_parts(n):
                    dve.wait_ge(hi_ready, n + 1)
                    for dst, hi, src in ((x_lo, x_hi, x_ps), (y_lo, y_hi, y_ps)):
                        last = dve.tensor_tensor(dst[:, :, :].rearrange("p k n -> p (k n)"), src[:, :],
                                                 hi[:, :, :].rearrange("p k n -> p (k n)").bitcast(F32), ALU.subtract)
                    last.then_inc(lo_ready, 1)

                norm_input(0, 0, 1)
                norm_input(1, 1, 1)
                lo_parts(0)
                dve.wait_ge(vec_loaded, 16 * 3)

                def body(t, s, b, _, i):
                    more = not isinstance(t, int)
                    last_block = isinstance(t, int) and t == TILES - 1
                    dve.wait_ge(res_ready, after(t))
                    dve.wait_ge(gate_done, t + 1)
                    dve.tensor_tensor(a[:, :], gate_ps[:, :], gate_bias[:, :], ALU.add).then_inc(z_ready, 1)
                    dve.wait_ge(bc_loaded, 16 * (b + 1))
                    dve.wait_ge(sig_ready, t + 1)
                    dve.tensor_tensor(a[:, :], a[:, :], bc[:, :], ALU.mult).then_inc(mixed, 1)
                    dve.wait_ge(mixed, t + 1)
                    dve.tensor_tensor(a[:, :], a[:, :], xn[s][:, :], ALU.add).then_inc(added, 1)
                    dve.wait_ge(added, t + 1)
                    n = post_no(t)
                    ln_statistics(dve, ln, n, a, P, st[s], mv[s])
                    if not last_block:
                        lo_parts(t + 1)
                    ln_apply(dve, ln, n, a[:, :], a[:, :], mv[s], rstd[s], P).then_inc(normed, 1)
                    dve.wait_ge(normed, t + 1)
                    dve.tensor_tensor(a[:, :], a[:, :], gamma[:, :], ALU.mult).then_inc(scaled, 1)
                    dve.wait_ge(scaled, t + 1)
                    dve.tensor_tensor(a[:, :], a[:, :], beta[:, :], ALU.add).then_inc(shifted, 1)
                    dve.wait_ge(sig2_ready, t + 1)
                    dve.tensor_tensor(a[:, :], a[:, :], c_[:, :], ALU.mult).then_inc(silu_done, 1)
                    dve.wait_ge(silu_done, t + 1)
                    dve.wait_ge(out_done, t + 1)
                    dve.tensor_tensor(a[:, :], out_ps[:, :], a[:, :], ALU.mult).then_inc(gated, 1)
                    dve.wait_ge(gated, after(t + 1))
                    dve.wait_ge(stored, landed(t))
                    dve.tensor_tensor(res[:, :], a[:, :], xt[s][:, :], ALU.add).then_inc(res_ready, 1)
                    if more:
                        norm_input(post_no(t) + 1, s, (TB // 2) * b + i + 2)
                tiles(dve, body)


def program(nc, x, Wq, Wk, Wv, Wo, in_gamma, in_beta, agg_w, agg_b, pn_gamma, pn_beta, d1_w, d1_b, d2_w, d2_b,
            bc_w, bc_b, gate_w, gate_b, out_gamma, out_beta, out):
    WT = nc.dram_tensor("WT", (O0 + O_TILES, P, 2 * C), F32, kind="Internal").ap()
    Y = nc.dram_tensor("Y", (B, T, C), F32, kind="Internal").ap()
    BC = nc.dram_tensor("BC", (B, C), F32, kind="Internal").ap()
    prepare_weights(nc, WT, Wq, Wk, Wv, Wo)
    attend(nc, WT, Y, BC, x, in_gamma, in_beta, agg_w, agg_b, pn_gamma, pn_beta, d1_w, d1_b, d2_w, d2_b,
           bc_w, bc_b)
    finish(nc, WT, Y, BC, x, gate_w, gate_b, out_gamma, out_beta, out)


_INS = ["L0_attn_x", "L0_attn_Wq", "L0_attn_Wk", "L0_attn_Wv", "L0_attn_Wo", "L0_ffn_in_gamma", "L0_ffn_in_beta",
        "L0_ffn_agg_w", "L0_ffn_agg_b", "L0_ffn_pn_gamma", "L0_ffn_pn_beta", "L0_ffn_d1_w", "L0_ffn_d1_b",
        "L0_ffn_d2_w", "L0_ffn_d2_b", "L0_ffn_bc_w", "L0_ffn_bc_b", "L0_ffn_gate_w", "L0_ffn_gate_b",
        "L0_ffn_out_gamma", "L0_ffn_out_beta"]
_OUTS = [((4, 1024, 1024), "float32")]


def kernel(**inputs):
    import numpy as _np
    import concourse.bacc as _bacc
    from concourse import mybir as _mybir
    from concourse.bass_utils import run_bass_kernel_spmd as _run

    nc = _bacc.Bacc("TRN2", target_bir_lowering=False, num_devices=1)
    arrays, args = {}, []
    for name in _INS:
        a = _np.ascontiguousarray(inputs[name])
        arrays[f"in_{name}_dram"] = a
        args.append(nc.dram_tensor(f"in_{name}_dram", a.shape, _mybir.dt.from_np(a.dtype), kind="ExternalInput").ap())
    for i, (shape, dtype) in enumerate(_OUTS):
        dt = _mybir.dt.from_np(_np.dtype(dtype))
        args.append(nc.dram_tensor(f"out_{i}_dram", shape, dt, kind="ExternalOutput").ap())
    program(nc, *args)
    r = _run(nc, [arrays], core_ids=[0])
    got = tuple(r.results[0][f"out_{i}_dram"] for i in range(len(_OUTS)))
    return got[0]
```

```python
from contextlib import ExitStack

import concourse.bass as bass
from concourse import mybir

F32 = mybir.dt.float32
F32R = mybir.dt.float32r
ACT = mybir.ActivationFunctionType
ALU = mybir.AluOpType
AX = mybir.AxisListType

P = 128
B, T, C = 4, 1024, 1024
HEADS, KV, HS = 16, 4, 64
WINDOW, SINK = 512, 4
HID = 4096
KB = C // P
TB = T // P
HB = HID // P
BANK = 512
WB = WINDOW // P
WIDE = (WB + 1) * P
NEG = -3.0e38
SCALE = HS ** -0.5
EPS_X, EPS_FFN = 1e-5, 1e-6
Q_TILES, K_TILES, V_TILES, O_TILES = 8, 2, 2, 8
K0 = Q_TILES
V0 = K0 + K_TILES
O0 = V0 + V_TILES
UNITS = 2 * 2 * TB
FW_BLOCKS = 4
FW_TILES = 8





def start_counted(eng, *sems, dma=False):
    for s in sems:
        eng.sem_inc(s, 16 if dma else 1)


def after(n):
    return n + 1


def landed(n):
    return 16 * n + 16


def blocks_of(qb):
    return min(qb + 1, WB + 1)


class LayerNormStats:

    def __init__(self, stats_done, var_done, rstd_done, eps_added, wait_over):
        self.wait_over = wait_over
        self.stats_done, self.var_done = stats_done, var_done
        self.rstd_done, self.eps_added = rstd_done, eps_added


def ln_statistics(dve, ln, n, src, rows, st, mv):
    for half in range(2):
        last = dve.bn_stats(st[0:rows, half, :], src[:, half * BANK:(half + 1) * BANK])
    last.then_inc(ln.stats_done, 1)
    dve.wait_ge(ln.stats_done, n + 1)
    dve.sem_inc(ln.wait_over, 1)
    dve.bn_aggr(mv[0:rows, :], st[0:rows, :, :]).then_inc(ln.var_done, 1)


def ln_rstd(pool, ln, n, mv, rstd, rows, eps, minus_half):
    pool.wait_ge(ln.var_done, n + 1)
    pool.tensor_tensor(rstd[0:rows, 1:2], mv[0:rows, 1:2], eps[0:rows, :], ALU.add).then_inc(ln.eps_added, 1)
    pool.wait_ge(ln.eps_added, n + 1)
    pool.tensor_tensor(rstd[0:rows, 0:1], rstd[0:rows, 1:2], minus_half[0:rows, :],
                       ALU.pow).then_inc(ln.rstd_done, 1)


def ln_apply(dve, ln, n, dst, src, mv, rstd, rows):
    dve.wait_ge(ln.rstd_done, n + 1)
    return dve.tensor_scalar(dst, src, mv[0:rows, 0:1], rstd[0:rows, 0:1], ALU.subtract, ALU.mult)


def prepare_weights(nc, WT, Wq, Wk, Wv):
    SLOTS = 4
    with ExitStack() as ctx:
        def sb(name, shape, dt):
            return ctx.enter_context(nc.sbuf_tensor(name, shape, dt))

        def sem(name):
            return ctx.enter_context(nc.semaphore(name))

        raw = [sb(f"w_raw{s}", [P, C], F32) for s in range(SLOTS)]
        split = [sb(f"w_split{s}", [P, 2, C], F32R) for s in range(SLOTS)]
        ident = sb("w_ident", [P, P], F32)
        turned = [ctx.enter_context(nc.psum_tensor(f"w_turned{s}", [P, C], F32)) for s in range(SLOTS)]
        zeroed, ident_ready = sem("w_zeroed"), sem("w_ident_ready")
        raw_loaded = [sem(f"w_raw_loaded{s}") for s in range(SLOTS)]
        split_stored = [sem(f"w_split_stored{s}") for s in range(SLOTS)]
        transposed, hi_ready, lo_ready = sem("w_transposed"), sem("w_hi_ready"), sem("w_lo_ready")

        def source(t):
            W, row = (Wq, t) if t < K0 else (Wk, t - K0) if t < V0 else (Wv, t - V0)
            return W[row * P:row * P + P, :]

        TURNS = O0 // SLOTS

        with nc.Block() as block:
            @block.sync
            def _(sp):
                for t in range(O0):
                    sp.wait_ge(lo_ready, t + 1)
                    sp.dma_start(WT[t, :, :], split[t % SLOTS][:, :, :].rearrange("p a n -> p (a n)").bitcast(F32)
                                 ).then_inc(split_stored[t % SLOTS], 16)
                for s in range(SLOTS):
                    sp.wait_ge(split_stored[s], 16 * TURNS)

            @block.gpsimd
            def _(pool):
                pool.memset(ident[:, :], 0.0).then_inc(zeroed, 1)
                pool.wait_ge(zeroed, 1)
                pool.affine_select(out=ident[:, :], in_=ident[:, :], compare_op=ALU.not_equal, fill=1.0,
                                   base=0, pattern=[[-1, P]], channel_multiplier=1).then_inc(ident_ready, 1)

            @block.tensor
            def _(pe):
                pe.wait_ge(ident_ready, 1)
                for t in range(O0):
                    s = t % SLOTS
                    pe.wait_ge(raw_loaded[s], 16 * (t // SLOTS) + 16)
                    if t >= SLOTS:
                        pe.wait_ge(lo_ready, t - SLOTS + 1)
                    for c in range(KB):
                        last = pe.transpose(turned[s][:, bass.ts(c, P)], raw[s][:, bass.ts(c, P)], ident[:, :])
                    last.then_inc(transposed, 1)

            @block.scalar
            def _(act):
                for t in range(SLOTS):
                    act.dma_start(raw[t][:, :], source(t)).then_inc(raw_loaded[t], 16)
                for t in range(O0):
                    s = t % SLOTS
                    act.wait_ge(transposed, t + 1)
                    if t >= SLOTS:
                        act.wait_ge(split_stored[s], 16 * (t // SLOTS))
                    act.activation(split[s][:, 0, :], turned[s][:, :], ACT.Copy).then_inc(hi_ready, 1)
                    if t + SLOTS < O0:
                        act.dma_start(raw[s][:, :], source(t + SLOTS)).then_inc(raw_loaded[s], 16)

            @block.vector
            def _(dve):
                for t in range(O0):
                    s = t % SLOTS
                    dve.wait_ge(hi_ready, t + 1)
                    dve.tensor_tensor(split[s][:, 1, :], turned[s][:, :], split[s][:, 0, :].bitcast(F32),
                                      ALU.subtract).then_inc(lo_ready, 1)


def attend(nc, WT, Y, BC, x, in_gamma, in_beta, agg_w, agg_b, pn_gamma, pn_beta, d1_w, d1_b, d2_w, d2_b,
           bc_w, bc_b):
    with ExitStack() as ctx:
        def sb(name, shape, dt=F32):
            return ctx.enter_context(nc.sbuf_tensor(name, shape, dt))

        def ps(name, cols):
            return ctx.enter_context(nc.psum_tensor(name, [P, cols], F32))

        def sem(name):
            return ctx.enter_context(nc.semaphore(name))

        def pt_view(tile):
            return tile.rearrange("p (k h q) -> p k h q", h=2, q=P)

        xn = [sb(f"xn{s}", [P, C]) for s in range(2)]
        x_hi = sb("x_hi", [P, KB, T], F32R)
        x_lo = sb("x_lo", [P, KB, T], F32R)
        w = sb("w", [P, 4, 2 * C], F32R)
        k_hi = sb("k_hi", [P, KV, TB, P + SINK], F32R)
        k_lo = sb("k_lo", [P, KV, TB, P + SINK], F32R)
        v = sb("v", [P, TB, KV, HS])
        v_cur = sb("v_cur", [P, TB, 2, HS], F32R)
        v_sink = sb("v_sink", [P, 2, HS], F32R)
        q = [sb(f"q{n}", [P, T], F32R) for n in range(4)]
        probs = [sb(f"probs{n}", [P, WIDE + SINK]) for n in range(3)]
        PT = (WB + 1) * 2 * P
        pt_hi = [pt_view(w[:, 2:4, :].rearrange("p s n -> p (s n)")[:, PT * n:PT * n + PT]) for n in range(2)]
        pt_lo = [pt_view(w[:, 2:4, :].rearrange("p s n -> p (s n)")[:, 2 * PT:3 * PT]),
                 pt_view(sb("pt_lo1", [P, PT], F32R)[:, :])]
        pt_sink = sb("pt_sink", [P, 2, P], F32R)
        mask = sb("mask", [P, WIDE + SINK])
        mask4 = sb("mask4", [P, WIDE])
        y = [sb(f"y{n}", [P, P]) for n in range(2)]
        neg_max, row_sum, inv_sum = sb("neg_max", [P, 4]), sb("row_sum", [P, 4]), sb("inv_sum", [P, 4])
        ident = sb("ident", [P, P])
        fold = sb("fold", [P, B])
        st = [sb(f"st{s}", [P, 2, 6]) for s in range(2)]
        mv = [sb(f"mv{s}", [P, 2]) for s in range(2)]
        rstd = [sb(f"rstd{s}", [P, 2]) for s in range(2)]
        eps_x, eps_ffn, minus_half = sb("eps_x", [P, 1]), sb("eps_ffn", [P, 1]), sb("minus_half", [P, 1])
        fw = [sb(f"fw{s}", [P, FW_BLOCKS, BANK]) for s in range(2)]
        rows = xn[1][:, 0:BANK]
        ffn_rows = sb("ffn_rows", [P, C])
        thought = ffn_rows[0:B, :]
        t_rows = ffn_rows[32:32 + B, :]
        bias_rows = ffn_rows[64:64 + B, :]
        affine = sb("affine", [P, 4, KB])
        d1_bias = sb("d1_bias", [P, HB])
        h_pre = sb("h_pre", [P, HB, B])
        cols = sb("cols", [P, HB * B + 32 - B])
        cols_view = cols[:, 0:HB * B].rearrange("p (k b) -> p k b", b=B)

        s_ps = [ps(f"s_ps{n}", 2 * BANK) for n in range(2)]
        t_ps = ps("t_ps", 2 * BANK)
        o_ps = ps("o_ps", BANK)
        j_ps = ps("j_ps", BANK)
        o_view = o_ps[:, 0:2 * P].rearrange("p (h q) -> p h q", h=2)
        f_cols = j_ps[:, 0:KB * B]
        f_hid = j_ps[:, 0:4 * B].rearrange("p (n b) -> p n b", b=B)

        small_loaded = sem("small_loaded")
        bias_loaded = sem("bias_loaded")
        last_loaded = sem("last_loaded")
        x_loaded = [sem(f"x_loaded{s}") for s in range(2)]
        w_loaded = [sem(f"w_loaded{s}") for s in range(2)]
        vw_loaded = sem("vw_loaded")
        fw_loaded = [sem(f"fw_loaded{s}") for s in range(2)]
        y_stored = [sem(f"y_stored{n}") for n in range(2)]
        bc_stored = sem("bc_stored")
        filled, masks_ready, ident_ready, fold_ready = (sem("filled"), sem("masks_ready"), sem("ident_ready"),
                                                        sem("fold_ready"))
        ln = LayerNormStats(sem("ln_stats"), sem("ln_var"), sem("ln_rstd"), sem("ln_eps"), sem("ln_wait_over"))
        xn_ready, x_turned, x_hi_ready, x_lo_ready = sem("xn_ready"), sem("x_turned"), sem("x_hi_r"), sem("x_lo_r")
        k_full, k_hi_ready, k_lo_ready = sem("k_full"), sem("k_hi_r"), sem("k_lo_r")
        k_sink_ready = sem("k_sink_r")
        v_full, v_ready = sem("v_full"), sem("v_ready")
        q_full, q_hi_ready, q_lo_ready = sem("q_full"), sem("q_hi_r"), sem("q_lo_r")
        scores_ready, masked, exp_done = sem("scores_ready"), sem("masked"), sem("exp_done")
        inv_ready, normed_act, normed_dve = sem("inv_ready"), sem("normed_act"), sem("normed_dve")
        turned_a, turned_b, pt_hi_a, pt_hi_b = sem("turned_a"), sem("turned_b"), sem("pt_hi_a"), sem("pt_hi_b")
        pt_lo_b, pt_ready = sem("pt_lo_b"), sem("pt_ready")
        v_hi_ready, v_lo_ready, v_sink_ready = sem("v_hi_r"), sem("v_lo_r"), sem("v_sink_r")
        sinks_zeroed, sink_wait_over = sem("sinks_zeroed"), sem("sink_wait_over")
        pv_done, y_half, y_ready = sem("pv_done"), sem("y_half"), sem("y_ready")
        fw_used, rows_ready, f_turned = sem("fw_used"), sem("rows_ready"), sem("f_turned")
        t_rows_ready, cols_ready, cols_scaled = sem("t_rows_ready"), sem("cols_ready"), sem("cols_scaled")
        hid_turned, hid_ready, gelu_done = sem("hid_turned"), sem("hid_ready"), sem("gelu_done")
        folded, biased, thought_ready = sem("folded"), sem("biased"), sem("thought_ready")
        last_normed, rows_zeroed, wait_over = sem("last_normed"), sem("rows_zeroed"), sem("wait_over")

        d1_view = d1_w.rearrange("(h k p) n -> h p k n", k=FW_BLOCKS, p=P)
        d2_view = d2_w.rearrange("(h k p) n -> h p k n", k=FW_BLOCKS, p=P)
        agg_view = agg_w.rearrange("(h k p) n -> h p k n", k=FW_BLOCKS, p=P)
        bc_view = bc_w.rearrange("(h k p) n -> h p k n", k=FW_BLOCKS, p=P)

        def unit(u):
            return u // (2 * TB), (u // 2) % TB, u % 2

        wide = [0] * (UNITS + 1)
        for u in range(UNITS):
            wide[u + 1] = wide[u] + (blocks_of(unit(u)[1]) > WB)
        Q_COPIED = {3: 1, 6: 2, 14: 3}
        LATEST = 14

        by_act = [u % 2 == 1 for u in range(UNITS)]
        act_before = [sum(by_act[:u]) for u in range(UNITS + 1)]
        dve_before = [u - act_before[u] for u in range(UNITS + 1)]

        HIDDEN_TILE = {17 + 4 * n + r: 2 * n + r for n in range(4) for r in range(2)}
        HIDDEN_COPIED = {18 + 4 * n: n for n in range(4)}
        HIDDEN_ADDED = {20 + 4 * n: n for n in range(4)}
        OUTPUT_TILE = {17 + 2 * t: t for t in range(FW_TILES)}
        OUTPUT_COPIED, OUTPUT_FOLDED, OUTPUT_ADDED = 32, 33, 34

        def ffn_tile(layer, u):
            return (HIDDEN_TILE if layer == 0 else OUTPUT_TILE).get(u)

        FW_FIRST = 4
        Q_LNS = 2
        LNS = TB + 1

        def chunks_before(b, layer, j):
            return 2 + b * 10 + (4 * j if layer == 0 else 8 + j)

        def loops(eng, start, hidden_start, output_start, body, end=None):
            with eng.Fori(0, B) as b:
                start(b)
                for layer in range(2):
                    if layer == 0:
                        hidden_start(b)
                    else:
                        output_start(b)
                    with eng.Fori(0, 2) as j:
                        body(b, layer, j, 2 * layer + j, 4 * b + 2 * layer + j)

        def nothing(b):
            return None

        with nc.Block() as block:
            @block.sync
            def _(sp):
                start_counted(sp, *y_stored, dma=True)
                sp.wait_ge(rows_zeroed, 1)
                sp.dma_start(thought[:, :], x[:, T - 1, :]).then_inc(last_loaded, 16)
                sp.dma_start(bias_rows[:, :], agg_b.partition_broadcast(B)).then_inc(bias_loaded, 16)
                with nc.allow_non_contiguous_dma(reason="small vectors, one element per partition"):
                    for n, vec in enumerate((in_gamma, in_beta, pn_gamma, pn_beta)):
                        sp.dma_start(affine[:, n, :], vec.rearrange("(k p) -> p k", p=P)).then_inc(small_loaded, 16)
                    sp.dma_start(d1_bias[:, :], d1_b.rearrange("(k p) -> p k", p=P)).then_inc(small_loaded, 16)

                def fw_load(view, n, half, count):
                    s = n % 2
                    sp.wait_ge(fw_used, count - 1)
                    sp.dma_start(fw[s][:, :, :], view[half, :, :, bass.ts(n_col[0], BANK)]).then_inc(fw_loaded[s], 16)

                n_col = [0]
                for n in range(4):
                    n_col[0] = n // 2
                    if n == 2:
                        for s in range(2):
                            sp.dma_start(w[:, s, :].bitcast(F32), WT[K0 + s, :, :]).then_inc(w_loaded[s], 16)
                    if n < 2:
                        sp.dma_start(fw[n][:, :, :], agg_view[n, :, :, 0:BANK]).then_inc(fw_loaded[n], 16)
                    else:
                        fw_load(agg_view, n, n - 2, n)

                def start(b):
                    sp.wait_ge(pv_done, after(2 * TB * 4 * b))
                    for s in range(2):
                        sp.dma_start(w[:, 2 + s, :].bitcast(F32), WT[V0 + s, :, :]).then_inc(vw_loaded, 16)
                    sp.wait_ge(k_full, 4 * b + 4)
                    for s in range(2):
                        sp.dma_start(w[:, s, :].bitcast(F32), WT[s, :, :]).then_inc(w_loaded[s], 16)

                def body(b, layer, j, g, it):
                    def load(tile):
                        s = tile % 2
                        count = FW_FIRST + FW_TILES * it + tile
                        sp.wait_ge(fw_used, count - 1)
                        if layer == 0:
                            src = d1_view[tile % 2, :, :, bass.ts(4 * j + tile // 2, BANK)]
                        else:
                            src = d2_view[tile, :, :, bass.ts(j, BANK)]
                        sp.dma_start(fw[s][:, :, :], src).then_inc(fw_loaded[s], 16)

                    load(0)
                    load(1)
                    sp.wait_ge(q_full, 4 * it + 2)
                    sp.dma_start(w[:, 0, :].bitcast(F32), WT[2 * g + 2, :, :]).then_inc(w_loaded[0], 16)
                    for u in range(UNITS + 4):
                        if u == 16:
                            sp.wait_ge(q_full, 4 * it + 4)
                            sp.dma_start(w[:, 1, :].bitcast(F32), WT[2 * g + 3, :, :]).then_inc(w_loaded[1], 16)
                        tile = ffn_tile(layer, u)
                        if tile is not None and tile + 2 < FW_TILES:
                            load(tile + 2)
                        if u >= 5 and u % 2 == 1:
                            n = (u - 5) // 2
                            pair, qb = n // TB, n % TB
                            sp.wait_ge(y_ready, after(2 * TB * it + n + 1))
                            sp.dma_start(Y[TB * b + qb, :, 2 * g + pair, :], y[n % 2][:, :]).then_inc(
                                y_stored[n % 2], 16)

                loops(sp, start, nothing, nothing, body)
                sp.wait_ge(thought_ready, 2 + 2 * B)
                sp.dma_start(bias_rows[:, :], bc_b.partition_broadcast(B)).then_inc(bias_loaded, 16)
                for n in range(4):
                    n_col[0] = n // 2
                    fw_load(bc_view, n, n % 2, FW_FIRST + FW_TILES * 4 * B + n)
                sp.wait_ge(thought_ready, 4 + 2 * B)
                for half in range(2):
                    sp.dma_start(BC[:, half, :], t_rows[:, :]).then_inc(bc_stored, 16)
                sp.wait_ge(bc_stored, 32)
                for n in range(2):
                    sp.wait_ge(y_stored[n], landed(TB * 4 * B))
                for s in range(2):
                    sp.wait_ge(w_loaded[s], 16 * (1 + 5 * B))

            @block.gpsimd
            def _(pool):
                pool.memset(ffn_rows[:, :], 0.0).then_inc(rows_zeroed, 1)
                pool.memset(ident[:, :], 0.0)
                pool.memset(mask[:, :], 0.0)
                pool.memset(mask4[:, :], 0.0)
                pool.memset(cols[:, :], 0.0)
                pool.memset(eps_x[:, :], EPS_X)
                pool.memset(eps_ffn[:, :], EPS_FFN)
                pool.memset(minus_half[:, :], -0.5).then_inc(filled, 1)
                pool.wait_ge(filled, 1)
                pool.affine_select(out=ident[:, :], in_=ident[:, :], compare_op=ALU.not_equal, fill=1.0,
                                   base=0, pattern=[[-1, P]], channel_multiplier=1).then_inc(ident_ready, 1)
                pool.tensor_copy(v_sink[:, :, :], mask[:, P:2 * P].rearrange("p (h d) -> p h d", d=HS))
                pool.tensor_copy(pt_sink[:, :, :], mask[:, P:3 * P].rearrange("p (h q) -> p h q", q=P)).then_inc(
                    sinks_zeroed, 1)
                for m in (mask, mask4):
                    pool.affine_select(out=m[:, 0:P], in_=m[:, 0:P], compare_op=ALU.is_ge, fill=NEG,
                                       base=-1, pattern=[[1, P]], channel_multiplier=-1)
                    pool.affine_select(out=m[:, WB * P:WIDE], in_=m[:, WB * P:WIDE], compare_op=ALU.is_ge, fill=NEG,
                                       base=0, pattern=[[-1, P]], channel_multiplier=1).then_inc(masks_ready, 1)
                pool.wait_ge(masks_ready, 2)
                pool.memset(mask4[:, 0:SINK], 0.0).then_inc(masks_ready, 1)

                ln_rstd(pool, ln, 0, mv[0], rstd[0], B, eps_x, minus_half)
                ln_rstd(pool, ln, 1, mv[1], rstd[1], B, eps_ffn, minus_half)

                def start(b):
                    def load(t):
                        if t == 1:
                            pool.wait_ge(thought_ready, 2 + 2 * b)
                        pool.wait_ge(x_turned, after(TB * b + max(t - 1, 0)))
                        pool.dma_start(xn[t % 2][:, :], x[b, bass.ts(t, P), :]).then_inc(x_loaded[t % 2], 16)

                    load(0)
                    load(1)
                    for t in range(TB):
                        if 2 <= t + 1 < TB and t >= 1:
                            load(t + 1)
                        ln_rstd(pool, ln, Q_LNS + LNS * b + t, mv[t % 2], rstd[t % 2], P, eps_x, minus_half)
                    pool.wait_ge(k_lo_ready, 4 * b + 2)
                    pool.sem_inc(sink_wait_over, 1)
                    for k in (k_hi, k_lo):
                        for block_no in range(WB + 1, TB):
                            last = pool.tensor_copy(k[:, :, block_no, P:P + SINK], k[:, :, 0, 0:SINK])
                    last.then_inc(k_sink_ready, 1)
                    ln_rstd(pool, ln, Q_LNS + LNS * b + TB, mv[0], rstd[0], B, eps_ffn, minus_half)

                def body(b, layer, j, g, it):
                    pool.wait_ge(sinks_zeroed, 1)
                    pool.wait_ge(v_lo_ready, it + 1)
                    pool.sem_inc(sink_wait_over, 1)
                    for quadrant in range(4):
                        last = pool.tensor_copy(v_sink[32 * quadrant:32 * quadrant + SINK, :, :],
                                                v_cur[0:SINK, 0, :, :])
                    last.then_inc(v_sink_ready, 1)

                loops(pool, start, nothing, nothing, body)

            @block.scalar
            def _(act):
                def copy_rows(tiles):
                    act.wait_ge(fw_used, tiles)
                    act.activation(rows[:, :], j_ps[:, :], ACT.Copy).then_inc(rows_ready, 1)

                for c in range(2):
                    copy_rows(2 * c + 2)
                act.wait_ge(thought_ready, 2)
                act.dma_start(bias_rows[:, :], d2_b.partition_broadcast(B)).then_inc(bias_loaded, 16)

                def start(b):
                    for t in range(TB + 1):
                        if t < TB:
                            act.wait_ge(x_turned, after(TB * b + t + 1))
                            act.activation(x_hi[:, :, bass.ts(t, P)],
                                           s_ps[t % 2][:, :].rearrange("p (k n) -> p k n", n=P),
                                           ACT.Copy).then_inc(x_hi_ready, 1)
                        if t >= 1:
                            act.wait_ge(v_full, TB * b + t)
                            o = BANK * ((t - 1) % 2)
                            act.activation(v[:, t - 1, :, :],
                                           t_ps[:, o:o + KV * HS].rearrange("p (g d) -> p g d", d=HS),
                                           ACT.Copy).then_inc(v_ready, 1)
                        for n in {5: (0, 1), TB - 1: (2, 3)}.get(t, ()):
                            k_copies(b, n)

                def k_copies(b, n):
                    m, ch = n % 2, n // 2
                    src = (j_ps, o_ps)[n % 2]
                    act.wait_ge(k_full, 4 * b + n + 1)
                    for head in range(2):
                        for half in range(2):
                            last = act.activation(k_hi[HS * half:HS * half + HS, 2 * m + head, 4 * ch:4 * ch + 4, 0:P],
                                                  src[HS * head:HS * head + HS, :].rearrange("p (k n) -> p k n", n=P),
                                                  ACT.Copy)
                    last.then_inc(k_hi_ready, 1)

                def q_copies(it, n):
                    pair, ch = n // 2, n % 2
                    src = s_ps[0][:, bass.ts(n, BANK)] if n < 2 else j_ps
                    act.wait_ge(q_full, 4 * it + n + 1)
                    for head in range(2):
                        h = slice(HS * head, HS * head + HS)
                        last = act.activation(q[2 * pair + head][h, bass.ts(ch, BANK)], src[h, 0:BANK], ACT.Copy)
                    last.then_inc(q_hi_ready, 1)

                def output_start(b):
                    act.wait_ge(hid_ready, after(8 * b + 8))
                    act.activation(cols_view[:, :, :], h_pre[:, :, :], ACT.Gelu).then_inc(gelu_done, 1)

                def body(b, layer, j, g, it):
                    act.wait_ge(v_ready, TB * b + TB)
                    act.wait_ge(pv_done, after(2 * TB * it))
                    act.activation(v_cur[:, :, 0, :], v[:, :, g, :], ACT.Copy).then_inc(v_hi_ready, 1)
                    q_copies(it, 0)
                    for s in range(UNITS + 4):
                        if s == LATEST:
                            q_copies(it, Q_COPIED[s])
                        if 2 <= s < UNITS + 2:
                            u = s - 2
                            _, qb, head = unit(u)
                            n, slot = u // 2, u // 2 % 2
                            if head == 0 and n >= 2:
                                act.wait_ge(pv_done, after(2 * TB * it + n - 1))
                            if blocks_of(qb) > WB:
                                act.wait_ge(turned_b, wide[UNITS] * it + wide[u + 1])
                                last = act.activation(pt_hi[slot][:, WB, head, :], t_ps[:, WB * P:WIDE], ACT.Copy)
                                if qb > WB:
                                    act.wait_ge(sinks_zeroed, 1)
                                    rows_ = slice(64 * slot, 64 * slot + SINK)
                                    last = act.activation(pt_sink[rows_, head, :], t_ps[0:SINK, WIDE:WIDE + P],
                                                          ACT.Copy)
                                last.then_inc(pt_hi_b, 1)
                            k = min(blocks_of(qb), WB)
                            act.wait_ge(turned_a, UNITS * it + u + 1)
                            act.activation(pt_hi[slot][:, 0:k, head, :],
                                           t_ps[:, 0:k * P].rearrange("p (k q) -> p k q", q=P),
                                           ACT.Copy).then_inc(pt_hi_a, 1)
                        if s in Q_COPIED and s != LATEST:
                            q_copies(it, Q_COPIED[s])
                        if 1 <= s < UNITS + 1 and by_act[s - 1]:
                            u = s - 1
                            _, qb, _ = unit(u)
                            n = blocks_of(qb) * P + (SINK if qb > WB else 0)
                            act.wait_ge(inv_ready, UNITS * it + u + 1)
                            act.activation(probs[u % 3][:, 0:n], probs[u % 3][:, 0:n], ACT.Copy,
                                           scale=inv_sum[:, u % 4:u % 4 + 1]).then_inc(normed_act, 1)
                        if s < UNITS:
                            _, qb, _ = unit(s)
                            n = blocks_of(qb) * P + (SINK if qb > WB else 0)
                            act.wait_ge(masked, UNITS * it + s + 1)
                            act.activation(probs[s % 3][:, 0:n], probs[s % 3][:, 0:n], ACT.Exp,
                                           bias=neg_max[:, s % 4:s % 4 + 1], scale=-1.0,
                                           accum_out=row_sum[:, s % 4:s % 4 + 1]).then_inc(exp_done, 1)
                        if s >= 5 and s % 2 == 1:
                            n = (s - 5) // 2
                            act.wait_ge(pv_done, after(2 * TB * it + n + 1))
                            act.wait_ge(y_stored[n % 2], landed(TB * it + n // 2))
                            for head in range(2):
                                last = act.activation(y[n % 2][HS * head:HS * head + HS, :],
                                                      o_view[HS * (1 - head):HS * (1 - head) + HS, head, :], ACT.Copy)
                            last.then_inc(y_half, 1)
                        if layer == 0 and s in HIDDEN_COPIED:
                            n = HIDDEN_COPIED[s]
                            copy_rows(FW_FIRST + FW_TILES * it + 2 * n + 2)
                        if layer == 1 and s == OUTPUT_COPIED:
                            copy_rows(FW_FIRST + FW_TILES * (it + 1))

                loops(act, start, nothing, output_start, body)
                for c in range(2):
                    copy_rows(FW_FIRST + FW_TILES * 4 * B + 2 * c + 2)

            @block.tensor
            def _(pe):
                start_counted(pe, x_turned)
                pe.wait_ge(ident_ready, 1)
                pe.wait_ge(fold_ready, 1)

                def turn_rows(p):
                    for k in range(KB):
                        last = pe.matmul(f_cols[:, B * k:B * k + B], ffn_rows[0:64, bass.ts(k, P)], ident[0:64, p:p + B],
                                         start=True, stop=True)
                    last.then_inc(f_turned, 1)

                def ffn_products(cols, first, tile, count, start, stop):
                    s = tile % 2
                    pe.wait_ge(fw_loaded[s], 16 * (count // 2) + 16)
                    for k in range(FW_BLOCKS):
                        last = pe.matmul(j_ps[32 * k:32 * k + 32, :], cols[:, bass.ds(B * (first + k), 32)], fw[s][:, k, :],
                                         start=start, stop=stop)
                    last.then_inc(fw_used, 1)

                def fold_rows(chunk):
                    pe.wait_ge(rows_ready, chunk + 1)
                    pe.matmul(j_ps[0:B, :], fold[:, :], rows[:, :], start=True, stop=True).then_inc(folded, 1)

                pe.wait_ge(t_rows_ready, 1)
                turn_rows(32)
                pe.wait_ge(cols_ready, 1)

                def small_product(cols, tiles_before, chunks_before_, thoughts_before):
                    for c in range(2):
                        if c == 1:
                            pe.wait_ge(thought_ready, thoughts_before + 1)
                        for half in range(2):
                            ffn_products(cols, FW_BLOCKS * half, half, tiles_before + 2 * c + half,
                                         half == 0, half == 1)
                        fold_rows(chunks_before_ + c)

                small_product(cols, 0, 0, 0)

                def proj(out, wslot, ch):
                    steps = []
                    for c in range(KB):
                        for wp, xs in ((0, x_hi), (0, x_lo), (1, x_hi)):
                            steps.append((w[:, wslot, wp * C + c * P:wp * C + c * P + P], xs[:, c, bass.ts(ch, BANK)],
                                          c == 0 and wp == 0 and xs is x_hi, c == KB - 1 and wp == 1))

                    def run(a, z):
                        last = None
                        for lhs, rhs, first, final in steps[a:z]:
                            last = pe.matmul(out, lhs, rhs, start=first, stop=final)
                        return last
                    return run

                STEPS = 3 * KB

                def start(b):
                    def turn(t):
                        pe.wait_ge(xn_ready, TB * b + t + 1)
                        if t >= 2:
                            pe.wait_ge(x_lo_ready, TB * b + t - 1)
                        for c in range(KB):
                            last = pe.transpose(s_ps[t % 2][:, bass.ts(c, P)], xn[t % 2][:, bass.ts(c, P)], ident[:, :])
                        last.then_inc(x_turned, 1)

                    def v_proj(t):
                        pe.wait_ge(x_lo_ready, TB * b + t + 1)
                        if t == 0:
                            pe.wait_ge(vw_loaded, 32 * b + 32)
                        if t >= 2:
                            pe.wait_ge(v_ready, TB * b + t - 1)
                        o = BANK * (t % 2)
                        for c in range(KB):
                            for xs, wp in ((x_hi, 0), (x_hi, 1), (x_lo, 0)):
                                last = pe.matmul(t_ps[:, o:o + KV * HS], xs[:, c, bass.ts(t, P)],
                                                 w[:, 2:4, wp * C + c * P:wp * C + c * P + P],
                                                 start=(c == 0 and xs is x_hi and wp == 0),
                                                 stop=(c == KB - 1 and xs is x_lo))
                        last.then_inc(v_full, 1)

                    def k_proj(n):
                        if n < 2:
                            pe.wait_ge(w_loaded[n], 16 * (5 * b) + 16)
                        if n == 0:
                            pe.wait_ge(thought_ready, 2 + 2 * b)
                        if n >= 2:
                            pe.wait_ge(k_lo_ready, 4 * b + n - 1)
                        out = (j_ps, o_ps)[n % 2]
                        proj(out[:, :], n % 2, n // 2)(0, STEPS).then_inc(k_full, 1)

                    for t in range(TB + 1):
                        if t < TB:
                            turn(t)
                        if t == TB:
                            pe.wait_ge(x_lo_ready, TB * b + TB)
                            k_proj(2)
                            k_proj(3)
                        if t >= 1:
                            v_proj(t - 1)
                        if t == 5:
                            k_proj(0)
                            k_proj(1)

                def hidden_start(b):
                    pe.wait_ge(t_rows_ready, 2 + b)
                    pe.wait_ge(k_lo_ready, 4 * b + 3)
                    turn_rows(32)

                def body(b, layer, j, g, it):
                    pe.wait_ge(w_loaded[0], 16 * (5 * b + g) + 32)
                    for ch in range(2):
                        proj(s_ps[0][:, bass.ts(ch, BANK)], 0, ch)(0, STEPS).then_inc(q_full, 1)
                    q_b = [proj(j_ps[:, :], 1, ch) for ch in range(2)]

                    def scores(u):
                        pair, qb, head = unit(u)
                        if u % 16 == 0:
                            pe.wait_ge(q_lo_ready, 4 * it + (1 if u == 0 else 4))
                        if u == TB:
                            pe.wait_ge(q_lo_ready, 4 * it + 2)
                        if u >= 2:
                            pe.wait_ge(masked, UNITS * it + u - 1)
                        n = blocks_of(qb)
                        lhs = q[2 * pair + head][:, bass.ts(qb, P)]
                        first = qb - n + 1
                        if qb == WB + 1 and layer == 0 and pair == 0 and head == 0:
                            pe.wait_ge(k_sink_ready, b + 1)
                        pieces = [(0, slice(first, first + min(n, WB)), slice(0, P))]
                        if n > WB:
                            pieces.append((BANK, slice(qb, qb + 1), slice(0, P + (SINK if qb > WB else 0))))
                        for o, blocks, keys in pieces:
                            width = (blocks.stop - blocks.start) * keys.stop
                            for part, k in enumerate((k_hi, k_lo)):
                                last = pe.matmul(s_ps[u % 2][:, o:o + width], lhs, k[:, g, blocks, keys],
                                                 start=part == 0, stop=part == 1)
                        last.then_inc(scores_ready, 1)

                    def turn_probs(u):
                        _, qb, _ = unit(u)
                        if by_act[u]:
                            pe.wait_ge(normed_act, act_before[UNITS] * it + act_before[u + 1])
                        else:
                            pe.wait_ge(normed_dve, dve_before[UNITS] * it + dve_before[u + 1])
                        if u == 0 and layer == 0:
                            pe.wait_ge(v_ready, TB * b + TB)
                        n = blocks_of(qb)
                        if n > WB:
                            if wide[u]:
                                pe.wait_ge(pt_lo_b, wide[UNITS] * it + wide[u])
                            last = pe.transpose(t_ps[:, bass.ts(WB, P)], probs[u % 3][:, bass.ts(WB, P)], ident[:, :])
                            if qb > WB:
                                last = pe.transpose(t_ps[0:SINK, WIDE:WIDE + P], probs[u % 3][:, WIDE:WIDE + SINK],
                                                    ident[:, :])
                            last.then_inc(turned_b, 1)
                        if u >= 1:
                            pe.wait_ge(pt_ready, UNITS * it + u)
                        for i in range(min(n, WB)):
                            last = pe.transpose(t_ps[:, bass.ts(i, P)], probs[u % 3][:, bass.ts(i, P)], ident[:, :])
                        last.then_inc(turned_a, 1)

                    def values(block_no):
                        _, qb, _ = unit(2 * block_no)
                        n, slot = blocks_of(qb), block_no % 2
                        if block_no == 0:
                            pe.wait_ge(v_sink_ready, it + 1)
                            if layer == 0:
                                pe.wait_ge(k_lo_ready, 4 * b + 4)
                        pe.wait_ge(pt_ready, UNITS * it + 2 * block_no + 2)
                        pe.wait_ge(y_ready, after(2 * TB * it + block_no))
                        for i in range(n):
                            for part in (pt_hi[slot], pt_lo[slot]):
                                last = pe.matmul(o_view[:, :, :], v_cur[:, qb - n + 1 + i, :, :], part[:, i, :, :],
                                                 start=(i == 0 and part is pt_hi[slot]),
                                                 stop=(i == n - 1 and qb <= WB and part is pt_lo[slot]))
                        if qb > WB:
                            rows_ = slice(64 * slot, 64 * slot + 32 + SINK)
                            last = pe.matmul(o_view[:, :, :], v_sink[rows_, :, :], pt_sink[rows_, :, :],
                                             start=False, stop=True)
                        last.then_inc(pv_done, 1)

                    def ffn(u):
                        tile = ffn_tile(layer, u)
                        if tile is not None:
                            count = FW_FIRST + FW_TILES * it + tile
                            if layer == 0:
                                if tile % 2 == 0 and tile:
                                    pe.wait_ge(hid_ready, after(8 * b + 4 * j + tile // 2))
                                ffn_products(cols, FW_BLOCKS * (tile % 2), tile, count, tile % 2 == 0, tile % 2 == 1)
                            else:
                                if tile == 0:
                                    pe.wait_ge(gelu_done, b + 1)
                                ffn_products(cols, FW_BLOCKS * tile, tile, count, tile == 0, tile == FW_TILES - 1)
                        if layer == 0 and u in HIDDEN_ADDED:
                            n = HIDDEN_ADDED[u]
                            pe.wait_ge(rows_ready, chunks_before(b, layer, j) + n + 1)
                            for i in range(4):
                                last = pe.matmul(f_hid[:, i, :], rows[:, bass.ts(i, P)], fold[:, :],
                                                 start=True, stop=True)
                            last.then_inc(hid_turned, 1)

                    for s in range(UNITS + 3):
                        if s < UNITS:
                            scores(s)
                        if 2 <= s < UNITS + 2:
                            turn_probs(s - 2)
                        if s < 16:
                            if s == 0:
                                pe.wait_ge(w_loaded[1], 16 * (5 * b + g) + 32)
                                if layer == 0:
                                    pe.wait_ge(cols_ready, 2 + b)
                                    pe.wait_ge(hid_ready, after(8 * b + 4 * j))
                                else:
                                    pe.wait_ge(hid_ready, after(8 * b + 8))
                                    pe.wait_ge(thought_ready, 2 + 2 * b + j)
                            if s == 8:
                                pe.wait_ge(q_lo_ready, 4 * it + 3)
                            if s % 8 < 6:
                                cuts = ((0, 5, 10, 15, 18, 21, STEPS), (0, 4, 8, 12, 16, 20, STEPS))[s // 8]
                                last = q_b[s // 8](cuts[s % 8], cuts[s % 8 + 1])
                                if s % 8 == 5:
                                    last.then_inc(q_full, 1)
                        else:
                            ffn(s)
                        if s >= 4 and s % 2 == 0:
                            values((s - 4) // 2)
                        if layer == 1 and s == OUTPUT_FOLDED:
                            fold_rows(chunks_before(b, layer, j))

                loops(pe, start, hidden_start, nothing, body)
                pe.wait_ge(thought_ready, 2 + 2 * B)
                turn_rows(0)
                pe.wait_ge(cols_ready, 2 + B)
                small_product(cols, FW_FIRST + FW_TILES * 4 * B, 2 + 10 * B, 2 + 2 * B)

            @block.vector
            def _(dve):
                start_counted(dve, y_ready, hid_ready, pv_done)
                dve.wait_ge(ident_ready, 1)
                dve.tensor_reduce(fold[:, :], ident[:, :].rearrange("p (j n) -> p n j", j=4)[:, 0:B, :], AX.X,
                                  ALU.add).then_inc(fold_ready, 1)

                def scale_cols(gamma, turns):
                    dve.wait_ge(f_turned, turns + 1)
                    for k in range(KB):
                        last = dve.tensor_scalar(cols_view[:, k, :], f_cols[:, B * k:B * k + B],
                                                 affine[:, gamma, k:k + 1], affine[:, gamma + 1, k:k + 1],
                                                 ALU.mult, ALU.add)
                    last.then_inc(cols_ready, 1)

                def add_rows(c, count, dst, carry):
                    part = bass.ts(c, BANK)
                    dve.wait_ge(folded, count + 1)
                    if carry is None:
                        dve.tensor_tensor(dst[:, part], j_ps[0:B, :], bias_rows[:, part],
                                          ALU.add).then_inc(thought_ready, 1)
                    else:
                        dve.tensor_tensor(rows[0:B, :], j_ps[0:B, :], bias_rows[:, part],
                                          ALU.add).then_inc(biased, 1)
                        dve.wait_ge(biased, count - 1)
                        dve.tensor_tensor(dst[:, part], carry[:, part], rows[0:B, :],
                                          ALU.add).then_inc(thought_ready, 1)

                dve.wait_ge(last_loaded, 16)
                ln_statistics(dve, ln, 0, thought, B, st[0], mv[0])
                ln_apply(dve, ln, 0, thought[:, :], thought[:, :], mv[0], rstd[0], B).then_inc(last_normed, 1)
                dve.wait_ge(last_normed, 1)
                ln_statistics(dve, ln, 1, thought, B, st[1], mv[1])
                ln_apply(dve, ln, 1, t_rows[:, :], thought[:, :], mv[1], rstd[1], B).then_inc(t_rows_ready, 1)
                dve.wait_ge(small_loaded, 16 * 5)
                dve.wait_ge(filled, 1)
                scale_cols(0, 0)
                dve.wait_ge(bias_loaded, 16)
                for c in range(2):
                    add_rows(c, c, thought, None)

                def start(b):
                    def stats(t):
                        dve.wait_ge(x_loaded[t % 2], 16 * (4 * b + t // 2) + 16)
                        ln_statistics(dve, ln, Q_LNS + LNS * b + t, xn[t % 2], P, st[t % 2], mv[t % 2])

                    def x_low(t):
                        dve.wait_ge(x_hi_ready, TB * b + t + 1)
                        dve.tensor_tensor(x_lo[:, :, bass.ts(t, P)],
                                          s_ps[t % 2][:, :].rearrange("p (k n) -> p k n", n=P),
                                          x_hi[:, :, bass.ts(t, P)].bitcast(F32), ALU.subtract).then_inc(x_lo_ready, 1)

                    stats(0)
                    for t in range(TB + 1):
                        if t < TB:
                            ln_apply(dve, ln, Q_LNS + LNS * b + t, xn[t % 2][:, :], xn[t % 2][:, :], mv[t % 2],
                                     rstd[t % 2], P).then_inc(xn_ready, 1)
                        if t >= 1:
                            x_low(t - 1)
                        if t + 1 < TB:
                            stats(t + 1)
                        if t == 6:
                            k_low(b, 0)
                            k_low(b, 1)
                    n = Q_LNS + LNS * b + TB
                    dve.wait_ge(thought_ready, 2 + 2 * b)
                    ln_statistics(dve, ln, n, thought, B, st[0], mv[0])
                    ln_apply(dve, ln, n, t_rows[:, :], thought[:, :], mv[0], rstd[0], B).then_inc(t_rows_ready, 1)
                    k_low(b, 2)
                    k_low(b, 3)

                def k_low(b, n):
                    m, ch = n % 2, n // 2
                    src = (j_ps, o_ps)[n % 2]
                    dve.wait_ge(k_hi_ready, 4 * b + n + 1)
                    for head in range(2):
                        h = slice(HS * head, HS * head + HS)
                        for half in range(2):
                            last = dve.tensor_tensor(
                                k_lo[HS * half:HS * half + HS, 2 * m + head, 4 * ch:4 * ch + 4, 0:P],
                                src[h, :].rearrange("p (k n) -> p k n", n=P),
                                k_hi[h, 2 * m + head, 4 * ch:4 * ch + 4, 0:P].bitcast(F32), ALU.subtract)
                    last.then_inc(k_lo_ready, 1)

                def q_low(it, n):
                    pair, ch = n // 2, n % 2
                    src = s_ps[0][:, bass.ts(n, BANK)] if n < 2 else j_ps
                    dve.wait_ge(q_hi_ready, 4 * it + n + 1)
                    for head in range(2):
                        hi = slice(HS * head, HS * head + HS)
                        lo = slice(HS * (1 - head), HS * (1 - head) + HS)
                        last = dve.tensor_tensor(q[2 * pair + head][lo, bass.ts(ch, BANK)], src[hi, 0:BANK],
                                                 q[2 * pair + head][hi, bass.ts(ch, BANK)].bitcast(F32), ALU.subtract)
                    last.then_inc(q_lo_ready, 1)

                def hidden_start(b):
                    dve.wait_ge(bias_loaded, 32)
                    scale_cols(2, 1 + b)

                def body(b, layer, j, g, it):
                    dve.wait_ge(v_hi_ready, it + 1)
                    dve.tensor_tensor(v_cur[:, :, 1, :], v[:, :, g, :], v_cur[:, :, 0, :].bitcast(F32),
                                      ALU.subtract).then_inc(v_lo_ready, 1)
                    q_low(it, 0)
                    for s in range(UNITS + 4):
                        if 1 <= s < UNITS + 1:
                            k = (s - 1) % 4
                            dve.wait_ge(exp_done, UNITS * it + s)
                            dve.reciprocal(inv_sum[:, k:k + 1], row_sum[:, k:k + 1]).then_inc(inv_ready, 1)
                        if s < UNITS:
                            _, qb, _ = unit(s)
                            n = blocks_of(qb) * P
                            if qb == WB:
                                m, hidden = mask4[:, 0:n], 0
                            else:
                                m = mask[:, WIDE - n:WIDE + (SINK if qb > WB else 0)]
                            width = n + (SINK if qb > WB else 0)
                            if s == 0:
                                dve.wait_ge(masks_ready, 3)
                            dve.wait_ge(scores_ready, UNITS * it + s + 1)
                            dve.sem_inc(wait_over, 1)
                            dve.tensor_tensor_reduce(out=probs[s % 3][:, 0:width], in0=s_ps[s % 2][:, 0:width], in1=m,
                                                     scale=-SCALE, scalar=-NEG, op0=ALU.add, op1=ALU.min,
                                                     accum_out=neg_max[:, s % 4:s % 4 + 1]).then_inc(masked, 1)
                        if s == LATEST:
                            q_low(it, Q_COPIED[s])
                        if 1 <= s < UNITS + 1 and not by_act[s - 1]:
                            u = s - 1
                            _, qb, _ = unit(u)
                            n = blocks_of(qb) * P + (SINK if qb > WB else 0)
                            dve.wait_ge(inv_ready, UNITS * it + s)
                            dve.tensor_scalar(probs[u % 3][:, 0:n], probs[u % 3][:, 0:n], inv_sum[:, u % 4:u % 4 + 1],
                                              None, ALU.mult).then_inc(normed_dve, 1)
                        if 2 <= s < UNITS + 2:
                            u = s - 2
                            _, qb, head = unit(u)
                            slot = u // 2 % 2
                            if blocks_of(qb) > WB:
                                dve.wait_ge(pt_hi_b, wide[UNITS] * it + wide[u + 1])
                                last = dve.tensor_tensor(pt_lo[slot][:, WB, head, :], t_ps[:, WB * P:WIDE],
                                                  pt_hi[slot][:, WB, head, :].bitcast(F32), ALU.subtract)
                                if qb > WB:
                                    hi = slice(64 * slot, 64 * slot + SINK)
                                    last = dve.tensor_tensor(pt_sink[64 * slot + 32:64 * slot + 32 + SINK, head, :],
                                                             t_ps[0:SINK, WIDE:WIDE + P],
                                                             pt_sink[hi, head, :].bitcast(F32), ALU.subtract)
                                last.then_inc(pt_lo_b, 1)
                            k = min(blocks_of(qb), WB)
                            dve.wait_ge(pt_hi_a, UNITS * it + u + 1)
                            dve.tensor_tensor(pt_lo[slot][:, 0:k, head, :],
                                              t_ps[:, 0:k * P].rearrange("p (k q) -> p k q", q=P),
                                              pt_hi[slot][:, 0:k, head, :].bitcast(F32),
                                              ALU.subtract).then_inc(pt_ready, 1)
                        if s >= 5 and s % 2 == 1:
                            n = (s - 5) // 2
                            dve.wait_ge(y_half, 2 * TB * it + n + 1)
                            for head in range(2):
                                h = slice(HS * head, HS * head + HS)
                                last = dve.tensor_tensor(y[n % 2][h, :], o_view[h, head, :], y[n % 2][h, :], ALU.add)
                            last.then_inc(y_ready, 1)
                        if s in Q_COPIED and s != LATEST:
                            q_low(it, Q_COPIED[s])
                        if layer == 0 and s in HIDDEN_ADDED:
                            n = HIDDEN_ADDED[s]
                            dve.wait_ge(hid_turned, 8 * b + 4 * j + n + 1)
                            for row in range(B):
                                last = dve.tensor_tensor(h_pre[:, bass.ds(16 * j + 4 * n, 4), row], f_hid[:, :, row],
                                                         d1_bias[:, bass.ds(16 * j + 4 * n, 4)], ALU.add)
                            last.then_inc(hid_ready, 1)
                        if layer == 1 and s == OUTPUT_ADDED:
                            add_rows(j, 2 + 2 * b + j, thought, thought)

                loops(dve, start, hidden_start, nothing, body)
                dve.wait_ge(f_turned, 2 + B)
                dve.tensor_copy(cols_view[:, 0:KB, :], f_cols.rearrange("p (k b) -> p k b", b=B)).then_inc(cols_ready, 1)
                dve.wait_ge(bias_loaded, 48)
                for c in range(2):
                    add_rows(c, 2 + 2 * B + c, t_rows, None)


def finish(nc, Wo, Y, BC, x, gate_w, gate_b, out_gamma, out_beta, out):
    TILES = B * TB
    with ExitStack() as ctx:
        def sb(name, shape, dt=F32):
            return ctx.enter_context(nc.sbuf_tensor(name, shape, dt))

        def ps(name):
            return ctx.enter_context(nc.psum_tensor(name, [P, C], F32))

        def sem(name):
            return ctx.enter_context(nc.semaphore(name))

        wo = sb("wo", [P, O_TILES, 2, KB, P], F32R)
        g_hi, g_lo = sb("g_hi", [P, KB, C], F32R), sb("g_lo", [P, KB, C], F32R)
        gate_bias, gamma, beta, bc = (sb(n, [P, C]) for n in ("gate_bias", "gamma", "beta", "bc"))
        xt = [sb(f"b_x{s}", [P, C]) for s in range(2)]
        xn = [sb(f"b_xn{s}", [P, C]) for s in range(2)]
        yt = [sb(f"b_y{s}", [P, C]) for s in range(2)]
        x_hi, x_lo = ([sb(f"{n}{s}", [P, KB, P], F32R) for s in range(2)] for n in ("bx_hi", "bx_lo"))
        y_hi, y_lo = sb("by_hi", [P, KB, P], F32R), sb("by_lo", [P, KB, P], F32R)
        a, res = sb("b_a", [P, C]), sb("b_res", [P, C])
        ident = sb("b_ident", [P, P])
        eps_x, eps_ffn, minus_half = sb("b_eps_x", [P, 1]), sb("b_eps_ffn", [P, 1]), sb("b_minus_half", [P, 1])
        st = [sb(f"b_st{s}", [P, 2, 6]) for s in range(2)]
        mv = [sb(f"b_mv{s}", [P, 2]) for s in range(2)]
        rstd = [sb(f"b_rstd{s}", [P, 2]) for s in range(2)]
        x_ps, gate_ps, out_ps = ps("x_ps"), ps("gate_ps"), ps("out_ps")

        raw = [yt[1], a, res, xn[1], gamma, beta]
        RAW = len(raw)
        raw_loaded = [sem(f"b_raw_loaded{s}") for s in range(RAW)]
        vec_loaded = sem("b_vec_loaded")
        bc_loaded = sem("b_bc_loaded")
        x_loaded = [sem(f"b_x_loaded{s}") for s in range(2)]
        y_loaded = [sem(f"b_y_loaded{s}") for s in range(2)]
        stored = sem("b_stored")
        filled, ident_ready, w_hi_ready, w_lo_ready = (sem("b_filled"), sem("b_ident_ready"), sem("b_w_hi"),
                                                       sem("b_w_lo"))
        wo_turned = sem("b_wo_turned")
        ln = LayerNormStats(sem("b_ln_stats"), sem("b_ln_var"), sem("b_ln_rstd"), sem("b_ln_eps"), sem("b_ln_wait_over"))
        xn_ready, turned = sem("b_xn_ready"), sem("b_turned")
        x_hi_ready, x_lo_ready, y_hi_ready, y_lo_ready = sem("bx_hi"), sem("bx_lo"), sem("by_hi"), sem("by_lo")
        gate_done, out_done = sem("b_gate_done"), sem("b_out_done")
        z_ready, sig_ready, mixed, added = sem("b_z"), sem("b_sig"), sem("b_mixed"), sem("b_added")
        normed, scaled, shifted, sig2_ready = sem("b_normed"), sem("b_scaled"), sem("b_shifted"), sem("b_sig2")
        silu_done, gated, res_ready = sem("b_silu"), sem("b_gated"), sem("b_res_ready")

        WEIGHTS = 2 * KB

        def post_no(t):
            return 2 * t + 2 if follows(t, 1) else 2 * TILES - 1

        def wo_flat(n, part):
            return wo[:, n, part, :, :].rearrange("p k m -> p (k m)")

        def wo_ps(n):
            return (gate_ps, out_ps)[n % 2]

        bc_rows = BC.rearrange("b h c -> (b h) c")
        x_flat = x.rearrange("b t c -> (b t) c")
        y_rows = Y.rearrange("t p k q -> (t p) (k q)")
        out_flat = out.rearrange("b t c -> (b t) c")

        GROUP = TB // 2

        def tiles(eng, body, start=None):
            with eng.Fori(0, TILES // GROUP - 1) as i:
                if start:
                    start(i)
                for s in range(GROUP):
                    body(GROUP * i + s, s % 2, 2 * i + s // 2, i if s == 0 else None)
            if start:
                start(TILES // GROUP - 1)
            for s in range(GROUP):
                body(TILES - GROUP + s, s % 2, (TILES - GROUP + s) // 2, TILES // GROUP - 1 if s == 0 else None)

        def follows(t, n):
            return not isinstance(t, int) or t + n < TILES

        with nc.Block() as block:
            @block.sync
            def _(sp):
                start_counted(sp, stored, dma=True)
                for s in range(2):
                    sp.dma_start(xt[s][:, :], x_flat[bass.ts(s, P), :]).then_inc(x_loaded[s], 16)
                sp.dma_start(yt[0][:, :], y_rows[0:P, :]).then_inc(y_loaded[0], 16)
                for n in range(WEIGHTS):
                    if n >= RAW:
                        sp.wait_ge(w_lo_ready, n - RAW + 1)
                    src = (gate_w, Wo)[n % 2]
                    sp.dma_start(raw[n % RAW][:, :], src[bass.ts(n // 2, P), :]).then_inc(raw_loaded[n % RAW], 16)
                sp.wait_ge(w_lo_ready, WEIGHTS)
                sp.dma_start(yt[1][:, :], y_rows[bass.ts(1, P), :]).then_inc(y_loaded[1], 16)
                for dst, vec in ((gate_bias, gate_b), (gamma, out_gamma), (beta, out_beta)):
                    sp.dma_start(dst[:, :], vec.partition_broadcast(P)).then_inc(vec_loaded, 16)

                def load_bc(group):
                    if not isinstance(group, int) or group:
                        sp.wait_ge(mixed, after(GROUP * group))
                    sp.dma_start(bc[:, :], bc_rows[bass.ds(group, 1), :].rearrange("a c -> (a c)")
                                 .partition_broadcast(P)).then_inc(bc_loaded, 16)

                def body(t, s, pair, group):
                    if follows(t, 2):
                        sp.wait_ge(y_lo_ready, after(t + 1))
                        sp.dma_start(yt[s][:, :], y_rows[bass.ds(P * (t + 2), P), :]).then_inc(y_loaded[s], 16)
                    sp.wait_ge(res_ready, after(t + 1))
                    if follows(t, 2):
                        sp.dma_start(xt[s][:, :], x_flat[bass.ds(P * (t + 2), P), :]).then_inc(x_loaded[s], 16)
                    sp.dma_start(out_flat[bass.ts(t, P), :], res[:, :]).then_inc(stored, 16)

                tiles(sp, body, load_bc)
                sp.wait_ge(stored, landed(TILES))

            @block.gpsimd
            def _(pool):
                pool.memset(ident[:, :], 0.0)
                pool.memset(eps_x[:, :], EPS_X)
                pool.memset(eps_ffn[:, :], EPS_FFN)
                pool.memset(minus_half[:, :], -0.5).then_inc(filled, 1)
                pool.wait_ge(filled, 1)
                pool.affine_select(out=ident[:, :], in_=ident[:, :], compare_op=ALU.not_equal, fill=1.0,
                                   base=0, pattern=[[-1, P]], channel_multiplier=1).then_inc(ident_ready, 1)
                ln_rstd(pool, ln, 0, mv[0], rstd[0], P, eps_x, minus_half)

                def body(t, s, pair, group):
                    if follows(t, 1):
                        ln_rstd(pool, ln, post_no(t) - 1, mv[1 - s], rstd[1 - s], P, eps_x, minus_half)
                    ln_rstd(pool, ln, post_no(t), mv[s], rstd[s], P, eps_ffn, minus_half)
                tiles(pool, body)

            @block.scalar
            def _(act):
                for n in range(WEIGHTS):
                    if n % 2 == 0:
                        act.wait_ge(raw_loaded[n % RAW], 16 * (n // RAW) + 16)
                        act.activation(g_hi[:, n // 2, :], raw[n % RAW][:, :], ACT.Copy).then_inc(w_hi_ready, 1)
                    else:
                        act.wait_ge(wo_turned, n // 2 + 1)
                        act.activation(wo_flat(n // 2, 0), wo_ps(n // 2)[:, :], ACT.Copy).then_inc(w_hi_ready, 1)

                def hi_part(dst, src, ready):
                    act.activation(dst[:, :, :].rearrange("p k n -> p (k n)"), src[:, :], ACT.Copy).then_inc(ready, 1)

                act.wait_ge(turned, 1)
                hi_part(x_hi[0], x_ps, x_hi_ready)
                act.wait_ge(y_loaded[0], 16)
                hi_part(y_hi, yt[0], y_hi_ready)

                def body(t, s, pair, group):
                    act.wait_ge(z_ready, t + 1)
                    act.activation(a[:, :], a[:, :], ACT.Sigmoid).then_inc(sig_ready, 1)
                    if follows(t, 1):
                        act.wait_ge(turned, t + 2)
                        hi_part(x_hi[1 - s], x_ps, x_hi_ready)
                    act.wait_ge(shifted, t + 1)
                    act.wait_ge(stored, landed(t))
                    act.activation(res[:, :], a[:, :], ACT.Sigmoid).then_inc(sig2_ready, 1)
                    if follows(t, 1):
                        act.wait_ge(y_loaded[1 - s], 16 * (pair + (s == 1)) + 16)
                        act.wait_ge(out_done, t + 1)
                        hi_part(y_hi, yt[1 - s], y_hi_ready)
                tiles(act, body)

            @block.tensor
            def _(pe):
                pe.wait_ge(ident_ready, 1)

                def turn(t, s):
                    pe.wait_ge(xn_ready, t + 1)
                    for c in range(KB):
                        last = pe.transpose(x_ps[:, bass.ts(c, P)], xn[s][:, bass.ts(c, P)], ident[:, :])
                    last.then_inc(turned, 1)

                def products(out_, hi, lo, w_hi, w_lo, blocks=range(KB)):
                    for c in blocks:
                        for lhs, rhs in ((hi, w_hi), (hi, w_lo), (lo, w_hi)):
                            for half in range(2):
                                last = pe.matmul(out_[:, bass.ts(half, BANK)], lhs[:, c, :], rhs(c, half),
                                                 start=(c == 0 and lhs is hi and rhs is w_hi),
                                                 stop=(c == KB - 1 and lhs is lo))
                    return last

                def gate_part(part):
                    return lambda c, half: part[:, c, bass.ts(half, BANK)]

                def wo_part(part):
                    return lambda c, half: wo[:, 4 * half:4 * half + 4, part, c, :]

                parts = [gate_part(g_hi), gate_part(g_lo), wo_part(0), wo_part(1)]
                for n in range(O_TILES):
                    i = 2 * n + 1
                    pe.wait_ge(raw_loaded[i % RAW], 16 * (i // RAW) + 16)
                    if n >= 2:
                        pe.wait_ge(w_lo_ready, i - 3)
                    for c in range(KB):
                        last = pe.transpose(wo_ps(n)[:, bass.ts(c, P)], raw[i % RAW][:, bass.ts(c, P)], ident[:, :])
                    last.then_inc(wo_turned, 1)
                turn(0, 0)
                pe.wait_ge(w_lo_ready, WEIGHTS)

                def body(t, s, pair, group):
                    pe.wait_ge(x_lo_ready, t + 1)
                    products(gate_ps, x_hi[s], x_lo[s], parts[0], parts[1]).then_inc(gate_done, 1)
                    pe.wait_ge(gated, after(t))
                    pe.wait_ge(y_lo_ready, after(t + 1))
                    products(out_ps, y_hi, y_lo, parts[2], parts[3], range(KB // 2))
                    if follows(t, 1):
                        turn(t + 1, 1 - s)
                    products(out_ps, y_hi, y_lo, parts[2], parts[3], range(KB // 2, KB)).then_inc(out_done, 1)
                tiles(pe, body)

            @block.vector
            def _(dve):
                start_counted(dve, res_ready, gated, y_lo_ready, mixed)

                def apply_input(n, s):
                    ln_apply(dve, ln, n, xn[s][:, :], xt[s][:, :], mv[s], rstd[s], P).then_inc(xn_ready, 1)

                dve.wait_ge(x_loaded[0], 16)
                ln_statistics(dve, ln, 0, xt[0], P, st[0], mv[0])
                apply_input(0, 0)
                for n in range(WEIGHTS):
                    dve.wait_ge(w_hi_ready, n + 1)
                    if n % 2 == 0:
                        dst, src, hi = g_lo[:, n // 2, :], raw[n % RAW][:, :], g_hi[:, n // 2, :]
                    else:
                        dst, src, hi = wo_flat(n // 2, 1), wo_ps(n // 2)[:, :], wo_flat(n // 2, 0)
                    dve.tensor_tensor(dst, src, hi.bitcast(F32), ALU.subtract).then_inc(w_lo_ready, 1)

                def lo_part(dst, src, hi, hi_ready, n, ready):
                    dve.wait_ge(hi_ready, n)
                    dve.tensor_tensor(dst[:, :, :].rearrange("p k n -> p (k n)"), src[:, :],
                                      hi[:, :, :].rearrange("p k n -> p (k n)").bitcast(F32),
                                      ALU.subtract).then_inc(ready, 1)

                lo_part(x_lo[0], x_ps, x_hi[0], x_hi_ready, 1, x_lo_ready)
                lo_part(y_lo, yt[0], y_hi, y_hi_ready, 1, y_lo_ready)
                dve.wait_ge(vec_loaded, 16 * 3)

                def body(t, s, pair, group):
                    dve.wait_ge(res_ready, after(t))
                    dve.wait_ge(gate_done, t + 1)
                    dve.tensor_tensor(a[:, :], gate_ps[:, :], gate_bias[:, :], ALU.add).then_inc(z_ready, 1)
                    n = post_no(t)
                    if follows(t, 1):
                        dve.wait_ge(x_loaded[1 - s], 16 * (pair + (s == 1)) + 16)
                        ln_statistics(dve, ln, n - 1, xt[1 - s], P, st[1 - s], mv[1 - s])
                    if group is not None:
                        dve.wait_ge(bc_loaded, 16 * group + 16)
                    dve.wait_ge(sig_ready, t + 1)
                    dve.tensor_tensor(a[:, :], a[:, :], bc[:, :], ALU.mult).then_inc(mixed, 1)
                    if follows(t, 1):
                        apply_input(n - 1, 1 - s)
                    dve.wait_ge(mixed, after(t + 1))
                    dve.tensor_tensor(a[:, :], a[:, :], xn[s][:, :], ALU.add).then_inc(added, 1)
                    dve.wait_ge(added, t + 1)
                    ln_statistics(dve, ln, n, a, P, st[s], mv[s])
                    if follows(t, 1):
                        lo_part(x_lo[1 - s], x_ps, x_hi[1 - s], x_hi_ready, t + 2, x_lo_ready)
                    ln_apply(dve, ln, n, a[:, :], a[:, :], mv[s], rstd[s], P).then_inc(normed, 1)
                    dve.wait_ge(normed, t + 1)
                    dve.tensor_tensor(a[:, :], a[:, :], gamma[:, :], ALU.mult).then_inc(scaled, 1)
                    dve.wait_ge(scaled, t + 1)
                    dve.tensor_tensor(a[:, :], a[:, :], beta[:, :], ALU.add).then_inc(shifted, 1)
                    dve.wait_ge(sig2_ready, t + 1)
                    dve.tensor_tensor(a[:, :], a[:, :], res[:, :], ALU.mult).then_inc(silu_done, 1)
                    dve.wait_ge(silu_done, t + 1)
                    dve.wait_ge(out_done, t + 1)
                    dve.tensor_tensor(a[:, :], out_ps[:, :], a[:, :], ALU.mult).then_inc(gated, 1)
                    if follows(t, 1):
                        lo_part(y_lo, yt[1 - s], y_hi, y_hi_ready, t + 2, y_lo_ready)
                    dve.wait_ge(gated, after(t + 1))
                    dve.tensor_tensor(res[:, :], a[:, :], xt[s][:, :], ALU.add).then_inc(res_ready, 1)
                tiles(dve, body)


def program(nc, x, Wq, Wk, Wv, Wo, in_gamma, in_beta, agg_w, agg_b, pn_gamma, pn_beta, d1_w, d1_b, d2_w, d2_b,
            bc_w, bc_b, gate_w, gate_b, out_gamma, out_beta, out):
    WT = nc.dram_tensor("WT", (O0, P, 2 * C), F32, kind="Internal").ap()
    Y = nc.dram_tensor("Y", (B * TB, P, KB, P), F32, kind="Internal").ap()
    BC = nc.dram_tensor("BC", (B, 2, C), F32, kind="Internal").ap()
    prepare_weights(nc, WT, Wq, Wk, Wv)
    attend(nc, WT, Y, BC, x, in_gamma, in_beta, agg_w, agg_b, pn_gamma, pn_beta, d1_w, d1_b, d2_w, d2_b,
           bc_w, bc_b)
    finish(nc, Wo, Y, BC, x, gate_w, gate_b, out_gamma, out_beta, out)


_INS = ["L0_attn_x", "L0_attn_Wq", "L0_attn_Wk", "L0_attn_Wv", "L0_attn_Wo", "L0_ffn_in_gamma", "L0_ffn_in_beta",
        "L0_ffn_agg_w", "L0_ffn_agg_b", "L0_ffn_pn_gamma", "L0_ffn_pn_beta", "L0_ffn_d1_w", "L0_ffn_d1_b",
        "L0_ffn_d2_w", "L0_ffn_d2_b", "L0_ffn_bc_w", "L0_ffn_bc_b", "L0_ffn_gate_w", "L0_ffn_gate_b",
        "L0_ffn_out_gamma", "L0_ffn_out_beta"]
_OUTS = [((4, 1024, 1024), "float32")]


def kernel(**inputs):
    import numpy as _np
    import concourse.bacc as _bacc
    from concourse import mybir as _mybir
    from concourse.bass_utils import run_bass_kernel_spmd as _run

    nc = _bacc.Bacc("TRN2", target_bir_lowering=False, num_devices=1)
    arrays, args = {}, []
    for name in _INS:
        a = _np.ascontiguousarray(inputs[name])
        arrays[f"in_{name}_dram"] = a
        args.append(nc.dram_tensor(f"in_{name}_dram", a.shape, _mybir.dt.from_np(a.dtype), kind="ExternalInput").ap())
    for i, (shape, dtype) in enumerate(_OUTS):
        dt = _mybir.dt.from_np(_np.dtype(dtype))
        args.append(nc.dram_tensor(f"out_{i}_dram", shape, dt, kind="ExternalOutput").ap())
    program(nc, *args)
    r = _run(nc, [arrays], core_ids=[0])
    got = tuple(r.results[0][f"out_{i}_dram"] for i in range(len(_OUTS)))
    return got[0]
```
